# Optimizing a Trainium2 kernel written in Bass

```python
import numpy as np
import jax
import jax.numpy as jnp

def _softmax(x, axis=-1):
    return jax.nn.softmax(x, axis=axis)

def _gelu(x):
    return jax.nn.gelu(x, approximate=True)

def _silu(x):
    return jax.nn.silu(x)

def _sigmoid(x):
    return jax.nn.sigmoid(x)

def _layernorm(x, axis=-1, eps=1e-05):
    m = jnp.mean(x, axis=axis, keepdims=True)
    v = jnp.var(x, axis=axis, keepdims=True)
    return (x - m) / jnp.sqrt(v + eps)

def _scatter_add(tgt, idx, src, axis=0):
    return tgt.at[idx].add(src)

def _segment_sum(src, seg, n):
    return jax.ops.segment_sum(src, seg, n)
kernel_name = 'mk_seq_preln_d1_jaxref_r8_eb6b20'

def setup_inputs(seed: int=0):
    np.random.seed(seed)
    _w = jnp.asarray

    def _L0_attn_setup():
        import jax, jax.numpy as jnp
        import numpy as np
        EMB = 128
        HEADS = 16
        HEAD_DIM = EMB // HEADS
        ROPE_BASE = 10000.0

        def rotate_half(x):
            x1 = x[..., ::2]
            x2 = x[..., 1::2]
            return jnp.stack((-x2, x1), axis=-1).reshape(x.shape)

        def rope_cos_sin(seq_len, head_dim):
            inv_freq = 1.0 / ROPE_BASE ** (jnp.arange(0, head_dim, 2, dtype=jnp.float32) / head_dim)
            pos = jnp.arange(seq_len, dtype=jnp.float32)
            freqs = jnp.outer(pos, inv_freq)
            emb = jnp.concatenate([freqs, freqs], -1)
            return (jnp.cos(emb)[None, None], jnp.sin(emb)[None, None])
        key = jax.random.key(seed)
        ks = jax.random.split(key, 5)
        B, S = (2, 256)
        x = jax.random.normal(ks[0], (B, S, EMB), dtype=jnp.float32)
        scale = EMB ** (-0.5)
        Wq = jax.random.normal(ks[1], (EMB, EMB), dtype=jnp.float32) * scale
        Wk = jax.random.normal(ks[2], (EMB, EMB), dtype=jnp.float32) * scale
        Wv = jax.random.normal(ks[3], (EMB, EMB), dtype=jnp.float32) * scale
        Wo = jax.random.normal(ks[4], (EMB, EMB), dtype=jnp.float32) * scale
        return {'x': x, 'Wq': Wq, 'Wk': Wk, 'Wv': Wv, 'Wo': Wo}
    _L0_attn_in = _L0_attn_setup()

    def _L0_ffn_setup():
        import jax, jax.numpy as jnp
        import numpy as np
        E = 16
        H = 128
        F = 256
        TOP_K = 1
        B, S = (2, 128)
        key = jax.random.key(seed)
        ks = jax.random.split(key, 7)
        s = 0.02
        return {'hidden_states': jax.random.normal(ks[0], (B, S, H), jnp.float32), 'w_router': jax.random.normal(ks[1], (E, H), jnp.float32) * s, 'gate_up_proj': jax.random.normal(ks[2], (E, H, 2 * F), jnp.float32) * s, 'down_proj': jax.random.normal(ks[3], (E, F, H), jnp.float32) * s, 'w_gate': jax.random.normal(ks[4], (F, H), jnp.float32) * s, 'w_up': jax.random.normal(ks[5], (F, H), jnp.float32) * s, 'w_down': jax.random.normal(ks[6], (H, F), jnp.float32) * s}
    _L0_ffn_in = _L0_ffn_setup()
    _d = {'L0_attn_x': _L0_attn_in['x'], 'L0_attn_Wq': _L0_attn_in['Wq'], 'L0_attn_Wk': _L0_attn_in['Wk'], 'L0_attn_Wv': _L0_attn_in['Wv'], 'L0_attn_Wo': _L0_attn_in['Wo'], 'L0_ffn_w_router': _L0_ffn_in['w_router'], 'L0_ffn_gate_up_proj': _L0_ffn_in['gate_up_proj'], 'L0_ffn_down_proj': _L0_ffn_in['down_proj'], 'L0_ffn_w_gate': _L0_ffn_in['w_gate'], 'L0_ffn_w_up': _L0_ffn_in['w_up'], 'L0_ffn_w_down': _L0_ffn_in['w_down']}
    _x0 = _d['L0_attn_x']
    _d['L0_attn_x'] = jax.random.normal(jax.random.fold_in(jax.random.key(seed), 1), (4, 512, 128), dtype=_x0.dtype)
    del _x0
    return _d

def reference(L0_attn_x, L0_attn_Wq, L0_attn_Wk, L0_attn_Wv, L0_attn_Wo, L0_ffn_w_router, L0_ffn_gate_up_proj, L0_ffn_down_proj, L0_ffn_w_gate, L0_ffn_w_up, L0_ffn_w_down):

    def _L0_attn_ref(x, Wq, Wk, Wv, Wo):
        import jax, jax.numpy as jnp
        import numpy as np
        EMB = 128
        HEADS = 16
        HEAD_DIM = EMB // HEADS
        ROPE_BASE = 10000.0

        def rotate_half(x):
            x1 = x[..., ::2]
            x2 = x[..., 1::2]
            return jnp.stack((-x2, x1), axis=-1).reshape(x.shape)

        def rope_cos_sin(seq_len, head_dim):
            inv_freq = 1.0 / ROPE_BASE ** (jnp.arange(0, head_dim, 2, dtype=jnp.float32) / head_dim)
            pos = jnp.arange(seq_len, dtype=jnp.float32)
            freqs = jnp.outer(pos, inv_freq)
            emb = jnp.concatenate([freqs, freqs], -1)
            return (jnp.cos(emb)[None, None], jnp.sin(emb)[None, None])
        B, S, E = x.shape

        def shape_heads(t):
            return t.reshape(B, S, HEADS, HEAD_DIM).transpose(0, 2, 1, 3)
        q = shape_heads(x @ Wq.T)
        k = shape_heads(x @ Wk.T)
        v = shape_heads(x @ Wv.T)
        cos, sin = rope_cos_sin(S, HEAD_DIM)
        q = q * cos + rotate_half(q) * sin
        k = k * cos + rotate_half(k) * sin
        scale = HEAD_DIM ** (-0.5)
        scores = jnp.einsum('bhqd,bhkd->bhqk', q, k) * scale
        causal = jnp.triu(jnp.ones((S, S), dtype=bool), k=1)
        scores = jnp.where(causal, -jnp.inf, scores)
        attn = jax.nn.softmax(scores, axis=-1)
        out = jnp.einsum('bhqk,bhkd->bhqd', attn, v)
        out = out.transpose(0, 2, 1, 3).reshape(B, S, E)
        return out @ Wo.T

    def _L0_ffn_ref(hidden_states, w_router, gate_up_proj, down_proj, w_gate, w_up, w_down):
        import jax, jax.numpy as jnp
        import numpy as np
        E = 16
        H = 128
        F = 256
        TOP_K = 1
        B, S = (2, 128)
        b, s, h = hidden_states.shape
        x = hidden_states.reshape(-1, h)
        logits = x @ w_router.T
        _, top_idx = jax.lax.top_k(logits, TOP_K)
        mask = jax.nn.one_hot(top_idx, E, dtype=logits.dtype).sum(axis=1)
        scores = jax.nn.sigmoid(logits) * mask
        masked_inputs = scores.T[:, :, None] * x[None, :, :]
        gate_up = jnp.einsum('eth,ehf->etf', masked_inputs, gate_up_proj)
        gate, up = jnp.split(gate_up, 2, axis=-1)
        expert_out = jnp.einsum('etf,efh->eth', up * jax.nn.silu(gate), down_proj)
        shared = jax.nn.silu(x @ w_gate.T) * (x @ w_up.T) @ w_down.T
        out = shared + expert_out.sum(axis=0)
        return out.reshape(b, s, h)
    x = L0_attn_x
    x = x + _L0_attn_ref(_layernorm(x, axis=-1), L0_attn_Wq, L0_attn_Wk, L0_attn_Wv, L0_attn_Wo)
    x = x + _L0_ffn_ref(_layernorm(x, axis=-1), L0_ffn_w_router, L0_ffn_gate_up_proj, L0_ffn_down_proj, L0_ffn_w_gate, L0_ffn_w_up, L0_ffn_w_down)
    return x

_drawn_inputs = setup_inputs


def setup_inputs(seed=0):
    import zlib

    import numpy as np

    out = dict(_drawn_inputs(seed))
    spreads = {}
    factors = {'L0_ffn_w_router': 8.0,
     'L0_ffn_gate_up_proj': 8.0,
     'L0_ffn_down_proj': 8.0,
     'L0_ffn_w_gate': 6.964,
     'L0_ffn_w_up': 6.929,
     'L0_ffn_w_down': 6.897}
    for name, (base, spread) in spreads.items():
        noise = np.random.default_rng([zlib.crc32(name.encode()), seed]).standard_normal(out[name].shape)
        drawn = base * np.exp(spread * noise) if base else spread * noise
        out[name] = jnp.asarray(drawn.astype(out[name].dtype))
    for name, factor in factors.items():
        out[name] = (out[name] * factor).astype(out[name].dtype)
    return out
```

```python
from contextlib import ExitStack

import concourse.bass as bass
from concourse import mybir

F32 = mybir.dt.float32
BF16 = mybir.dt.bfloat16
I32 = mybir.dt.int32
ALU = mybir.AluOpType
ACT = mybir.ActivationFunctionType
AX = mybir.AxisListType

P = 128
B, S, E = 4, 512, 128
H, D = 16, 8
NE, F = 16, 256
T = B * S // P
TB = S // P
HU = 4
UB = H // HU
U = B * UB
SCALE = float(D) ** -0.5
EPS = 1e-5
PARTS = 6
KS = PARTS * D
MROW = 64
KM = MROW + 3 * HU
VC = 32
NT = B * S // P + NE
ROW = E + 1
NOBODY = 1 << 20
RING = 4

CHUNKS = [(3, h, 1) for h in range(4)] + [(2, h, 1) for h in range(4)] + [(1, 0, 2), (1, 2, 2), (0, 0, 4)]
NC = len(CHUNKS)
PT_OFF = [0, HU * 512, HU * (512 + 384), HU * (512 + 384 + 256)]
PT_LEN = HU * (512 + 384 + 256 + 128)
LAST_CHUNK = [3, 7, 9, 10]


def width(block):
    return P * (block + 1)


def extras(u):
    b, g = divmod(u, UB)
    out = []
    if 0 < u <= U:
        out += [(1, "pv", (u - 1, 2)), (2, "pv", (u - 1, 3)), (4 if u % UB == 0 else 5, "ott", u - 1)]
    if g == 0 and 0 < b < B:
        out += [(3, "v", b)]
    if u + 1 < U:
        out += [(4, "mt", u + 1)]
    if u < U:
        out += [(6, "pv", (u, 0)), (10, "pv", (u, 1))]
    if g == 0 and b + 1 < B:
        out += [(at, "proj", (b + 1, i)) for i, at in enumerate((0, 2, 6, 8))]
    if g == 3 and b + 2 < B:
        out += [(8, "xn1t", b + 2)]
    if g == 0 and b > 0:
        out += [(8, "attnt", b - 1), (10, "wo", b - 1)]
    if g == 1 and b > 0:
        out += [(7, "xn2t", b - 1), (9, "logits", b - 1)]
    return sorted(out, key=lambda x: x[0])


STEPS = U + 2
PROLOGUE = [("xn1t", 0)] + [("proj", (0, i)) for i in range(4)] + [("v", 0), ("xn1t", 1), ("mt", 0)]
ORDER = PROLOGUE + [(t, a) for u in range(STEPS) for _, t, a in extras(u)]
P0_USES = [x for x in ORDER if x[0] in ("xn1t", "v", "mt", "attnt", "xn2t")]
P1_USES = [x for x in ORDER if x[0] in ("proj", "ott", "wo", "logits")]


def p0(task, arg):
    return P0_USES.index((task, arg))


def p1(task, arg):
    return P1_USES.index((task, arg))


def block_kernel(nc, x_in, wq, wqs, wk, wks, wv, wo, w_router, w_gu, w_dn, w_sh, w_shd,
                 cos_in, sin_in, ident_in, identb_in, mask_in, sel_in, rank_in, small_in, out):
    q_scr = nc.dram_tensor("q_scr", [2, KS, H, S], BF16)
    k_scr = nc.dram_tensor("k_scr", [2, KS, H, S], BF16)
    rows_scr = nc.dram_tensor("rows_scr", [NT * P, ROW], F32)
    y_scr = nc.dram_tensor("y_scr", [B * S, E], F32)
    x_dram = x_in.rearrange("b (t p) d -> b p t d", p=P)
    out_dram = out.rearrange("b (t p) d -> b p t d", p=P)

    with ExitStack() as ctx:
        def sb(name, shape, dt=F32):
            return ctx.enter_context(nc.sbuf_tensor(name, shape, dt))

        def sem(name):
            return ctx.enter_context(nc.semaphore(name))

        def bank(name):
            return ctx.enter_context(nc.psum_tensor(name, [P, 512], F32))

        x = sb("x", [P, T, E])
        qst = sb("qst", [P, H, S], BF16)
        kst = sb("kst", [P, H, S], BF16)
        pt = sb("pt", [P, 2, PT_LEN])
        wgu_sb = sb("wgu_sb", [P, NE, 2 * F])
        wdn_sb = sb("wdn_sb", [P, NE, 2, E])
        vaug = sb("vaug", [P, TB, H, VC])
        xn2t = sb("xn2t", [P, B * S])
        rows = sb("rows", [P, T, ROW])
        xnt = sb("xnt", [P, 2, S])
        xn1 = sb("xn1", [P, TB, E])
        xn2 = sb("xn2", [P, TB, E])
        cos_sb = sb("cos_sb", [P, S])
        sin_sb = sb("sin_sb", [P, S])
        t1 = sb("t1", [P, 2, S])
        t2 = sb("t2", [P, 2, S])
        parts = sb("parts", [P, 6, S], BF16)
        ots = sb("ots", [P, S])
        attn = sb("attn", [P, TB, H * D])
        attnt = sb("attnt", [P, S])
        w_att = sb("w_att", [P, 6, E])
        wr_sb = sb("wr_sb", [P, NE])
        wsh_sb = sb("wsh_sb", [P, 2 * F])
        wshd_sb = sb("wshd_sb", [P, 2, E])
        ident = sb("ident", [P, P])
        identb = sb("identb", [P, P], BF16)
        mask = sb("mask", [P, HU, P], BF16)
        rankc = sb("rankc", [P, 3 * P], BF16)
        small = sb("small", [P, 4 * NE + 2 * NT])
        mx = sb("mx", [P, 2, TB, HU])
        mres = sb("mres", [P, TB, HU])
        mparts = sb("mparts", [P, TB, 3, HU], BF16)
        m12 = sb("m12", [3 * HU, S], BF16)
        stats = sb("stats", [P, TB, 6])
        mv = sb("mv", [P, TB, 2])
        var = sb("var", [P, 2, TB])
        rstd = sb("rstd", [P, 2, TB])
        half = sb("half", [P, TB])
        rc = sb("rc", [P, TB, HU])
        lg = sb("lg", [P, TB, NE])
        eq = sb("eq", [P, TB, NE])
        mx4 = sb("mx4", [P, TB])
        c4 = sb("c4", [P, TB])
        th = sb("th", [P, TB])
        sg4 = sb("sg4", [P, TB])
        onehot = sb("onehot", [P, T, NE], BF16)
        zrow = sb("zrow", [P, ROW])
        cmp16 = sb("cmp16", [NE, NE])
        tsum = sb("tsum", [NE, 1])
        tsb = sb("tsb", [NE, P], BF16)
        base = sb("base", [P, 2 * NE])
        cmpt = sb("cmpt", [1, NT, NE])
        expf = sb("expf", [1, NT])
        expi = sb("expi", [1, NT], I32)
        rk = sb("rk", [P, T, NE])
        posf = sb("posf", [P, T])
        posi = sb("posi", [P, T], I32)
        ids = sb("ids", [P, NT], I32)
        shg = pt[:, 0, 0:1024].rearrange("p (c n) -> p c n", c=2)
        shh = pt[:, 0, 1024:3072].rearrange("p (r c n) -> p r c n", r=2, c=2)
        xt = pt[:, 0, 3072:3328].rearrange("p (r n) -> p r n", r=2)
        sg = pt[:, 0, 3328:3840].rearrange("p (r n) -> p r n", r=2)
        hh = pt[:, 0, 3840:4352].rearrange("p (r n) -> p r n", r=2)
        ht = pt[:, 0, 4352:4864].rearrange("p (r c n) -> p r c n", r=2, c=2)
        yl = pt[:, 1, 0:2048].rearrange("p (t d) -> p t d", t=T)
        yt = pt[:, 1, 2048:2560].rearrange("p (r n) -> p r n", r=RING)
        xin = pt[:, 1, 2560:2560 + RING * ROW].rearrange("p (r n) -> p r n", r=RING)

        a_bank = [bank("a0"), bank("a1")]
        b_bank = [bank("b0"), bank("b1"), bank("b2")]
        ot_bank = bank("ot")
        p0_bank = bank("p0")
        p1_bank = bank("p1")
        mt_view = p0_bank[0:3 * HU, 0:S // 2].bitcast(BF16)

        x_in_sem = [sem(f"x_loaded{b}") for b in range(B)]
        w_loaded = sem("w_loaded")
        c_loaded = sem("c_loaded")
        wexp_loaded = sem("wexp_loaded")
        sel_loaded = sem("sel_loaded")
        zeros_done = sem("zeros_done")
        vones_done = sem("vones_done")
        half_done = sem("half_done")
        zrow_done = sem("zrow_done")
        table_cleared = sem("table_cleared")
        ids_done = sem("ids_done")
        var_ready = sem("var_ready")
        rstd_ready = sem("rstd_ready")
        xn1_ready = sem("xn1_ready")
        xn2_ready = sem("xn2_ready")
        p0_full = sem("p0_full")
        p0_read = sem("p0_read")
        p1_full = sem("p1_full")
        p1_read = sem("p1_read")
        rope_ready = sem("rope_ready")
        split_ready = sem("split_ready")
        split_step = sem("split_step")
        parts_sent = sem("parts_sent")
        slot_loaded = [sem(f"slot_loaded{g}") for g in range(UB)]
        a_full = sem("a_full")
        a_read = sem("a_read")
        b_full = sem("b_full")
        b_read = sem("b_read")
        masked = sem("masked")
        pv_done = sem("pv_done")
        ot_read = sem("ot_read")
        mparts_ready = sem("mparts_ready")
        mrow_loaded = [sem("mrow_loaded0"), sem("mrow_loaded1")]
        norm_done = sem("norm_done")
        tanh_ready = sem("tanh_ready")
        mx4_ready = sem("mx4_ready")
        rows_ready = sem("rows_ready")
        onehot_ready = sem("onehot_ready")
        rank_full = sem("rank_full")
        tsb_ready = sem("tsb_ready")
        base_full = sem("base_full")
        experts_ready = sem("experts_ready")
        pos_ready = sem("pos_ready")
        scattered = sem("scattered")
        sh_full = sem("sh_full")
        sh_silu = sem("sh_silu")
        sh_mul = sem("sh_mul")
        shd_full = sem("shd_full")
        base_done = sem("base_done")
        xin_loaded = [sem(f"xin_loaded{i}") for i in range(RING)]
        xt_full = sem("xt_full")
        xt_ready = sem("xt_ready")
        ids_ready = sem("ids_ready")
        h_full = sem("h_full")
        silu_ready = sem("silu_ready")
        hh_ready = sem("hh_ready")
        ht_full = sem("ht_full")
        ht_ready = sem("ht_ready")
        y_full = sem("y_full")
        y_ready = sem("y_ready")
        y_sent = [sem(f"y_sent{i}") for i in range(RING)]
        yl_loaded = [sem(f"yl_loaded{b}") for b in range(B)]
        final_ready = sem("final_ready")
        stored = sem("stored")
        v_chain = sem("v_chain")
        v_copied = sem("v_copied")

        block = ctx.enter_context(nc.Block())

        @block.sync
        def _(sp):
            for b in range(B):
                sp.dma_start(x[:, b * TB:(b + 1) * TB, :], x_dram[b]).then_inc(x_in_sem[b], 16)
                if b == 0:
                    sp.dma_start(ident[:], ident_in).then_inc(w_loaded, 16)
                    for i, w in enumerate((wq, wqs, wk, wks, wv, wo)):
                        sp.dma_start(w_att[:, i, :], w).then_inc(w_loaded, 16)
                    sp.dma_start(cos_sb[:], cos_in).then_inc(w_loaded, 16)
                    sp.dma_start(sin_sb[:], sin_in).then_inc(w_loaded, 16)
                    sp.dma_start(identb[:], identb_in).then_inc(w_loaded, 16)
                    sp.dma_start(mask[:], mask_in).then_inc(w_loaded, 16)
            sp.wait_ge(zeros_done, 2)
            sp.dma_start(kst[MROW:KM, :, :], sel_in).then_inc(sel_loaded, 16)

            def send_parts(n):
                par = n % 2
                sp.wait_ge(split_ready, 2 * (n + 1))
                q_to = q_scr.ap()[par].rearrange("(r d) h t -> (d h) r t", d=D)
                k_to = k_scr.ap()[par].rearrange("(r d) h t -> (d h) r t", d=D)
                for to, r0, c, rep in ((q_to, 0, 0, 3), (q_to, 3, 1, 2), (q_to, 5, 2, 1)):
                    sp.dma_start(to[:, r0:r0 + rep, :],
                                 parts[:, c:c + 1, :].broadcast_to([P, rep, S])).then_inc(parts_sent, 16)
                for to, r0, c, n_c in ((k_to, 0, 3, 3), (k_to, 3, 3, 2), (k_to, 5, 3, 1)):
                    sp.dma_start(to[:, r0:r0 + n_c, :], parts[:, c:c + n_c, :]).then_inc(parts_sent, 16)
                sp.wait_ge(parts_sent, 96 * (n + 1))

            def load_slot(n, g):
                if n > 0:
                    sp.wait_ge(b_full, NC * (UB * (n - 1) + g + 1))
                hs = slice(HU * g, HU * g + HU)
                sp.dma_start(qst[0:KS, hs, :], q_scr.ap()[n % 2, :, hs, :]).then_inc(slot_loaded[g], 16)
                sp.dma_start(kst[0:KS, hs, :], k_scr.ap()[n % 2, :, hs, :]).then_inc(slot_loaded[g], 16)

            def load_maxima(u):
                g = u % UB
                sp.wait_ge(p0_read, p0("mt", u) + 1)
                if u >= UB:
                    sp.wait_ge(b_full, NC * (u - UB + 1))
                sp.dma_start(qst[MROW:KM, HU * g:HU * g + HU, :],
                             m12[:, :].rearrange("p (o s) -> p o s", o=1).broadcast_to([3 * HU, HU, S])
                             ).then_inc(mrow_loaded[u % 2], 16)

            send_parts(0)
            for g in range(UB):
                load_slot(0, g)
            sp.dma_start(wr_sb[:], w_router).then_inc(c_loaded, 16)
            sp.dma_start(rankc[:], rank_in).then_inc(c_loaded, 16)
            sp.dma_start(small[:], small_in).then_inc(c_loaded, 16)
            load_maxima(0)
            sp.wait_ge(zrow_done, 2)
            sp.dma_start(rows_scr.ap().rearrange("(t p) c -> p t c", p=P),
                         zrow[:, :].rearrange("p (o c) -> p o c", o=1).broadcast_to([P, NT, ROW])
                         ).then_inc(table_cleared, 16)
            for u in range(U):
                b, g = divmod(u, UB)
                if g > 0 and b + 1 < B:
                    if g == 1:
                        if u + 1 < U:
                            load_maxima(u + 1)
                        send_parts(b + 1)
                        load_slot(b + 1, 0)
                    else:
                        load_slot(b + 1, g - 1)
                if g == 0 and b > 0:
                    load_slot(b, UB - 1)
                if u + 1 < U and not (g == 1 and b + 1 < B):
                    load_maxima(u + 1)
                sp.dma_start(wgu_sb[:, u, :], w_gu[u]).then_inc(wexp_loaded, 16)
                sp.dma_start(wdn_sb[:, u, :, :], w_dn[u].rearrange("(c p) h -> p c h", p=P)).then_inc(wexp_loaded, 16)
            sp.dma_start(wsh_sb[:], w_sh).then_inc(wexp_loaded, 16)
            sp.dma_start(wshd_sb[:], w_shd.rearrange("(c p) h -> p c h", p=P)).then_inc(wexp_loaded, 16)

            sp.wait_ge(scattered, 16 * T)

            def load_rows(r, k, first):
                if not first:
                    sp.wait_ge(xt_full, r * RING + (k - RING + 1))
                    sp.wait_ge(ids_ready, r * RING + (k - RING + 1))
                sp.dma_start(xin[:, k, :], rows_scr.ap()[bass.ds(r * (RING * P) + k * P, P), :]
                             ).then_inc(xin_loaded[k], 16)

            for k in range(RING):
                load_rows(0, k, True)
            with sp.Fori(1, NT // RING) as r:
                for k in range(RING):
                    load_rows(r, k, False)

            for k in range(RING):
                sp.wait_ge(y_sent[k], 16 * (NT // RING))
            for b in range(B):
                sp.dma_start(yl[:, b * TB:(b + 1) * TB, :],
                             y_scr.ap().rearrange("(b t p) d -> b p t d", b=B, p=P)[b]).then_inc(yl_loaded[b], 16)
            for b in range(B):
                sp.wait_ge(final_ready, b + 1)
                sp.dma_start(out_dram[b], x[:, b * TB:(b + 1) * TB, :]).then_inc(stored, 16)
            sp.wait_ge(stored, 16 * B)

        @block.tensor
        def _(pe):
            def a_chunk(u, i):
                block_, h0, n = CHUNKS[i]
                w, g, c = width(block_), u % UB, NC * u + i
                if i == 0:
                    pe.wait_ge(slot_loaded[g], 32 * (u // UB + 1))
                if c >= 2:
                    pe.wait_ge(a_read, c - 1)
                to = a_bank[c % 2]
                for j in range(n):
                    h = HU * g + h0 + j
                    pe.matmul(to[:, j * w:(j + 1) * w], qst[0:KS, h, block_ * P:(block_ + 1) * P],
                              kst[0:KS, h, 0:w], start=(j == 0), stop=False, skip_group_check=True)
                diag = to[:, 0:n * w].rearrange("p (j w) -> p j w", j=n)[:, :, w - P:w]
                pe.matmul(diag, identb[:, :], mask[:, 0:n, :], start=False, stop=True,
                          skip_group_check=True).then_inc(a_full, 1)

            def b_chunk(u, i):
                block_, h0, n = CHUNKS[i]
                w, g, c, kt = width(block_), u % UB, NC * u + i, 3 - block_
                if i == 0:
                    pe.wait_ge(mrow_loaded[u % 2], 16 * (u // 2 + 1))
                    if u < 1:
                        pe.wait_ge(sel_loaded, 16)
                if c >= 3:
                    pe.wait_ge(b_read, c - 2)
                to = b_bank[c % 3]
                for j in range(n):
                    h = HU * g + h0 + j
                    mm = pe.matmul(to[:, j * w:(j + 1) * w], kst[0:KM, h, kt * P:(kt + 1) * P],
                                   qst[0:KM, h, kt * P:S], start=True, stop=True)
                mm.then_inc(b_full, 1)

            def transposes(to, src):
                for t in range(TB):
                    mm = pe.transpose(to[:, t * P:(t + 1) * P], src[:, t, :], ident[:, :])
                return mm

            def task(name, arg):
                if (name, arg) in P0_USES:
                    if p0(name, arg) > 0:
                        pe.wait_ge(p0_read, p0(name, arg))
                if (name, arg) in P1_USES:
                    if p1(name, arg) > 0:
                        pe.wait_ge(p1_read, p1(name, arg))
                if name == "xn1t":
                    pe.wait_ge(xn1_ready, arg + 1)
                    transposes(p0_bank, xn1).then_inc(p0_full, 1)
                elif name == "proj":
                    n, i = arg
                    pe.wait_ge(p0_read, p0("xn1t", n) + 1)
                    pe.matmul(p1_bank[:, :], w_att[:, i, :], xnt[:, n % 2, :], start=True,
                              stop=True).then_inc(p1_full, 1)
                elif name == "v":
                    for t in range(TB):
                        mm = pe.matmul(p0_bank[:, t * P:(t + 1) * P], xnt[:, arg % 2, t * P:(t + 1) * P],
                                       w_att[:, 4, :], start=True, stop=True)
                    mm.then_inc(p0_full, 1)
                elif name == "mt":
                    pe.wait_ge(mparts_ready, arg + 1)
                    for t in range(TB):
                        mm = pe.transpose(mt_view[:, t * P:(t + 1) * P],
                                          mparts[:, t, :, :].rearrange("p c h -> p (c h)"), identb[:, :])
                    mm.then_inc(p0_full, 1)
                elif name == "pv":
                    u, kt = arg
                    g, w, off = u % UB, S - kt * P, PT_OFF[kt]
                    pe.wait_ge(masked, TB * u + kt + 1)
                    if kt == 0:
                        pe.wait_ge(v_copied, u // UB + 1)
                        if u > 0:
                            pe.wait_ge(ot_read, u)
                    for j in range(HU):
                        mm = pe.matmul(ot_bank[32 * j:32 * j + VC, kt * P:S], vaug[:, kt, HU * g + j, :],
                                       pt[:, u % 2, off + j * w:off + (j + 1) * w],
                                       start=(kt == 0), stop=(kt == TB - 1), tile_position=(0, 32 * j))
                    mm.then_inc(pv_done, 1)
                elif name == "ott":
                    pe.wait_ge(ot_read, arg + 1)
                    transposes(p1_bank, ots[:, :].rearrange("p (t q) -> p t q", t=TB)).then_inc(p1_full, 1)
                elif name == "attnt":
                    pe.wait_ge(norm_done, UB * (arg + 1))
                    transposes(p0_bank, attn).then_inc(p0_full, 1)
                elif name == "wo":
                    pe.wait_ge(p0_read, p0("attnt", arg) + 1)
                    for t in range(TB):
                        mm = pe.matmul(p1_bank[:, t * P:(t + 1) * P], attnt[:, t * P:(t + 1) * P],
                                       w_att[:, 5, :], start=True, stop=True)
                    mm.then_inc(p1_full, 1)
                elif name == "xn2t":
                    pe.wait_ge(xn2_ready, arg + 1)
                    transposes(p0_bank, xn2).then_inc(p0_full, 1)
                elif name == "logits":
                    pe.wait_ge(p0_read, p0("xn2t", arg) + 1)
                    pe.wait_ge(c_loaded, 48)
                    for t in range(TB):
                        c = arg * TB + t
                        mm = pe.matmul(p1_bank[:, t * NE:(t + 1) * NE], xn2t[:, c * P:(c + 1) * P],
                                       wr_sb[:, :], start=True, stop=True)
                    mm.then_inc(p1_full, 1)

            pe.wait_ge(w_loaded, 16 * 11)
            for name, arg in PROLOGUE:
                if name == "mt":
                    for i in range(NC):
                        a_chunk(0, i)
                    task(name, arg)
                    for i in range(NC):
                        a_chunk(1, i)
                else:
                    task(name, arg)
            for u in range(STEPS):
                todo = extras(u)
                for i in range(NC):
                    if u < U:
                        b_chunk(u, i)
                    if u + 2 < U:
                        a_chunk(u + 2, i)
                    for after, name, arg in todo:
                        if after == i:
                            task(name, arg)

            def shared_up(b):
                if b == 0:
                    pe.wait_ge(wexp_loaded, 32 * U + 32)
                for c in range(2):
                    if b > 0:
                        pe.wait_ge(sh_silu, 2 * (b - 1) + c + 1)
                    pe.matmul(a_bank[c][:, :], wsh_sb[:, c * P:(c + 1) * P], xn2t[:, b * S:(b + 1) * S],
                              start=True, stop=True).then_inc(sh_full, 1)
                for c in range(2):
                    if b > 0:
                        pe.wait_ge(sh_mul, 2 * (b - 1) + c + 1)
                    pe.matmul(b_bank[c][:, :], wsh_sb[:, F + c * P:F + (c + 1) * P],
                              xn2t[:, b * S:(b + 1) * S], start=True, stop=True).then_inc(sh_full, 1)

            def shared_down(b):
                pe.wait_ge(sh_mul, 2 * b + 2)
                if b > 0:
                    pe.wait_ge(base_done, b)
                for t in range(TB):
                    for c in range(2):
                        mm = pe.matmul(b_bank[2][:, t * P:(t + 1) * P], shh[:, b % 2, c, t * P:(t + 1) * P],
                                       wshd_sb[:, c, :], start=(c == 0), stop=(c == 1))
                mm.then_inc(shd_full, 1)

            def ranks():
                pe.wait_ge(onehot_ready, B)
                pe.wait_ge(p0_read, len(P0_USES))
                pe.wait_ge(p1_read, len(P1_USES))
                r = p1_bank[:, 0:T * NE].rearrange("p (t e) -> p t e", e=NE)
                pe.matmul(r, rankc[:, 0:P], onehot[:, :, :], start=True, stop=False, skip_group_check=True)
                for t in range(T - 1):
                    pe.matmul(r[:, t + 1:T, :], rankc[:, P:2 * P],
                              onehot[:, t:t + 1, :].broadcast_to([P, T - 1 - t, NE]),
                              start=False, stop=(t == T - 2), skip_group_check=True)
                for t in range(T):
                    mm = pe.matmul(p0_bank[0:NE, 0:NE], onehot[:, t, :], rankc[:, P:P + NE],
                                   start=(t == 0), stop=(t == T - 1))
                mm.then_inc(rank_full, 1)
                pe.wait_ge(tsb_ready, 1)
                pe.matmul(p0_bank[:, 0:2 * NE], tsb[:, :], rankc[0:NE, 2 * P:2 * P + 2 * NE],
                          start=True, stop=True).then_inc(base_full, 1)

            shared_up(0)
            ranks()
            for b in range(1, B):
                shared_up(b)
                shared_down(b - 1)
            shared_down(B - 1)

            x_bank, h_bank, ht_bank, y_bank = [p0_bank, p1_bank], a_bank, b_bank[0:2], [b_bank[2], ot_bank]

            def tile_transpose(r, k, fill=False):
                pe.wait_ge(xin_loaded[k % RING], 16 * (r + k // RING + 1))
                if not fill:
                    pe.wait_ge(xt_ready, r * RING + (k - 1))
                pe.transpose(x_bank[k % 2][:, 0:P], xin[:, k % RING, 0:E], ident[:, :]).then_inc(xt_full, 1)

            def tile_up(r, k, fill=False):
                e = pe.value_load(expi[0:1, bass.ds(r * RING + k, 1)], min_val=0, max_val=NE - 1)
                pe.wait_ge(xt_ready, r * RING + (k + 1))
                if not fill:
                    pe.wait_ge(hh_ready, r * RING + (k - 1))
                pe.matmul(h_bank[k % 2][:, :], xt[:, k % 2, :],
                          wgu_sb[:, bass.ds(e, 1), :].rearrange("p o f -> p (o f)"),
                          start=True, stop=True).then_inc(h_full, 1)

            def tile_hidden(r, k, fill=False):
                pe.wait_ge(hh_ready, r * RING + (k + 1))
                if not fill:
                    pe.wait_ge(ht_ready, r * RING + (k - 1))
                for c in range(2):
                    mm = pe.transpose(ht_bank[k % 2][:, c * P:(c + 1) * P], hh[:, k % 2, c * P:(c + 1) * P],
                                      ident[:, :])
                mm.then_inc(ht_full, 1)

            def tile_down(r, k, fill=False):
                e = pe.value_load(expi[0:1, bass.ds(r * RING + k, 1)], min_val=0, max_val=NE - 1)
                pe.wait_ge(ht_ready, r * RING + (k + 1))
                if not fill:
                    pe.wait_ge(y_ready, r * RING + (k - 1))
                for c in range(2):
                    mm = pe.matmul(y_bank[k % 2][:, 0:E], ht[:, k % 2, c, :],
                                   wdn_sb[:, bass.ds(e, 1), c, :].rearrange("p o f -> p (o f)"),
                                   start=(c == 0), stop=(c == 1))
                mm.then_inc(y_full, 1)

            pe.wait_ge(experts_ready, 1)
            pe.wait_ge(base_done, B)
            pe.wait_ge(pos_ready, 1)
            for k in range(RING + 4):
                tile_transpose(0, k, k < 2)
                if k >= 1:
                    tile_up(0, k - 1, k - 1 < 2)
                if k >= 2:
                    tile_hidden(0, k - 2, k - 2 < 2)
                if k >= 3:
                    tile_down(0, k - 3, k - 3 < 2)
            with pe.Fori(2, NT // RING) as r:
                for k in range(RING):
                    tile_transpose(r, k)
                    tile_up(r, k - 1)
                    tile_hidden(r, k - 2)
                    tile_down(r, k - 3)
            end = NT // RING
            tile_up(end, -1)
            tile_hidden(end, -2)
            tile_down(end, -3)
            tile_hidden(end, -1)
            tile_down(end, -2)
            tile_down(end, -1)

        @block.scalar
        def _(act):
            def exp_chunk(u, i):
                block_, h0, n = CHUNKS[i]
                w, c, kt = width(block_), NC * u + i, 3 - block_
                act.wait_ge(b_full, c + 1)
                if i == 0 and u >= 2:
                    act.wait_ge(pv_done, TB * (u - 1))
                off = PT_OFF[kt] + h0 * w
                nc.scalar.activation(pt[:, u % 2, off:off + n * w], b_bank[c % 3][:, 0:n * w], ACT.Exp,
                                     scale=SCALE).then_inc(b_read, 1)

            def task(name, arg):
                if name == "pv":
                    u, kt = arg
                    if kt == TB - 1:
                        act.wait_ge(pv_done, TB * (u + 1))
                        if u > 0:
                            act.wait_ge(p1_full, p1("ott", u - 1) + 1)
                        nc.scalar.copy(ots[:, :], ot_bank[:, :]).then_inc(ot_read, 1)
                    return
                if (name, arg) not in P0_USES:
                    return
                act.wait_ge(p0_full, p0(name, arg) + 1)
                if name == "xn1t":
                    nc.scalar.copy(xnt[:, arg % 2, :], p0_bank[:, :]).then_inc(p0_read, 1)
                elif name == "v":
                    if arg > 0:
                        act.wait_ge(pv_done, TB * UB * arg)
                    act.wait_ge(vones_done, 2)
                    nc.scalar.copy(vaug[:, :, :, 0:D],
                                   p0_bank[:, :].rearrange("p (t h d) -> p t h d", t=TB, d=D)).then_inc(v_copied, 1)
                    act.wait_ge(v_copied, arg + 1)
                    act.sem_inc(p0_read, 1)
                elif name == "mt":
                    if arg > 0:
                        act.wait_ge(mrow_loaded[(arg - 1) % 2], 16 * ((arg - 1) // 2 + 1))
                    nc.scalar.copy(m12[:, :], mt_view).then_inc(p0_read, 1)
                elif name == "attnt":
                    nc.scalar.copy(attnt[:, :], p0_bank[:, :]).then_inc(p0_read, 1)
                elif name == "xn2t":
                    nc.scalar.copy(xn2t[:, arg * S:(arg + 1) * S], p0_bank[:, :]).then_inc(p0_read, 1)

            def gate(b):
                act.wait_ge(mx4_ready, b + 1)
                if b > 0:
                    act.wait_ge(rows_ready, b)
                nc.scalar.activation(th[:, :], mx4[:, :], ACT.Tanh, scale=0.5).then_inc(tanh_ready, 1)

            for name, arg in PROLOGUE:
                task(name, arg)
            for u in range(STEPS):
                b, g = divmod(u, UB)
                todo = extras(u)
                for i in range(NC):
                    if u < U:
                        exp_chunk(u, i)
                    for after, name, arg in todo:
                        if min(after + 1, NC - 1) == i:
                            task(name, arg)
                    if g == 2 and b > 0 and i == 2:
                        gate(b - 1)
            gate(B - 1)
            for b in range(B):
                for c in range(2):
                    act.wait_ge(sh_full, 4 * b + c + 1)
                    if b > 0:
                        act.wait_ge(sh_mul, 2 * (b - 1) + c + 1)
                    nc.scalar.activation(shg[:, c, :], a_bank[c][:, :], ACT.Silu).then_inc(sh_silu, 1)

            def tile_xt(r, k, fill=False):
                act.wait_ge(xt_full, r * RING + (k + 1))
                if not fill:
                    act.wait_ge(h_full, r * RING + (k - 1))
                nc.scalar.copy(xt[:, k % 2, :], [p0_bank, p1_bank][k % 2][:, 0:P]).then_inc(xt_ready, 1)

            def tile_silu(r, k, fill=False):
                act.wait_ge(h_full, r * RING + (k + 1))
                if not fill:
                    act.wait_ge(hh_ready, r * RING + (k - 1))
                nc.scalar.activation(sg[:, k % 2, :], a_bank[k % 2][:, 0:F], ACT.Silu).then_inc(silu_ready, 1)

            def tile_y(r, k, fill=False):
                act.wait_ge(y_full, r * RING + (k + 1))
                if not fill:
                    act.wait_ge(y_sent[k % RING], 16 * (r + k // RING))
                nc.scalar.copy(yt[:, k % RING, :], [b_bank[2], ot_bank][k % 2][:, 0:E]).then_inc(y_ready, 1)

            for k in range(RING + 4):
                tile_xt(0, k, k < 2)
                if k >= 1:
                    tile_silu(0, k - 1, k - 1 < 2)
                if k >= 3:
                    tile_y(0, k - 3, k - 3 < RING)
            with act.Fori(2, NT // RING) as r:
                for k in range(RING):
                    tile_xt(r, k)
                    tile_silu(r, k - 1)
                    tile_y(r, k - 3)
            end = NT // RING
            tile_silu(end, -1)
            for k in range(-3, 0):
                tile_y(end, k)

        @block.vector
        def _(dve):
            count = [0]

            def mark(ins):
                count[0] += 1
                ins.then_inc(v_chain, 1)
                return count[0]

            def after(n):
                dve.wait_ge(v_chain, n)

            def link(ins):
                after(mark(ins))

            def reduce_chunk(u, i):
                block_, h0, n = CHUNKS[i]
                w, c = width(block_), NC * u + i
                dve.wait_ge(a_full, c + 1)
                nc.vector.tensor_reduce(mx[:, u % 2, block_, h0:h0 + n],
                                        a_bank[c % 2][:, 0:n * w].rearrange("p (j w) -> p j w", j=n),
                                        AX.X, ALU.max).then_inc(a_read, 1)

            split_mark = [0]

            def split_maxima(u, i):
                m = mx[:, u % 2, :, :]
                if i > 0:
                    after(split_mark[0])
                if i == 0:
                    dve.wait_ge(a_read, NC * (u + 1))
                    if u > 0:
                        dve.wait_ge(p0_full, p0("mt", u - 1) + 1)
                    ins = nc.vector.tensor_scalar(mparts[:, :, 0, :], m, -1.0, None, ALU.mult)
                elif i == 1:
                    ins = nc.vector.scalar_tensor_tensor(out=mres[:, :, :], in0=m, scalar=-1.0,
                                                         in1=mparts[:, :, 0, :], op0=ALU.mult, op1=ALU.subtract)
                elif i == 2:
                    ins = nc.vector.tensor_copy(mparts[:, :, 1, :], mres[:, :, :])
                else:
                    nc.vector.tensor_tensor(mparts[:, :, 2, :], mres[:, :, :], mparts[:, :, 1, :],
                                            ALU.subtract).then_inc(mparts_ready, 1)
                    return
                split_mark[0] = mark(ins)

            ln_count = [0]

            def ln_stats(n, which):
                k = ln_count[0]
                ln_count[0] += 1
                if which == 0:
                    dve.wait_ge(x_in_sem[n], 16)
                for t in range(TB):
                    m = mark(nc.vector.bn_stats(stats[:, t, :], x[:, n * TB + t, :]))
                after(m)
                for t in range(TB):
                    m = mark(nc.vector.bn_aggr(mv[:, t, :], stats[:, t, :]))
                after(m)
                nc.vector.tensor_scalar(var[:, k % 2, :], mv[:, :, 1], EPS, None, ALU.add).then_inc(var_ready, 1)

            def ln_apply(n, which):
                k = ln_count[0] - 1
                dve.wait_ge(rstd_ready, k + 1)
                to, ready = (xn1, xn1_ready) if which == 0 else (xn2, xn2_ready)
                if n > 0:
                    if which == 0:
                        dve.wait_ge(p0_full, p0("xn1t", n - 1) + 1)
                    else:
                        dve.wait_ge(rows_ready, n)
                for t in range(TB):
                    ins = nc.vector.tensor_scalar(to[:, t, :], x[:, n * TB + t, :], mv[:, t, 0:1],
                                                  rstd[:, k % 2, t:t + 1], ALU.subtract, ALU.mult)
                ins.then_inc(ready, 1)

            def rope(n, i):
                qk, part = divmod(i, 2)
                dve.wait_ge(p1_full, p1("proj", (n, i)) + 1)
                if n > 0 and part == 0:
                    dve.wait_ge(split_ready, 2 * n)
                to, tab = ((t1, cos_sb), (t2, sin_sb))[part]
                nc.vector.tensor_tensor(to[:, qk, :], p1_bank[:, :], tab[:, :], ALU.mult).then_inc(p1_read, 1)

            def split_here(qk):
                dve.wait_ge(p1_read, 2 * qk + 2)
                a, r = t1[:, qk, :], t2[:, qk, :]
                c = 3 * qk
                link(nc.vector.tensor_tensor(a, a, r, ALU.add))
                link(nc.vector.tensor_copy(parts[:, c, :], a))
                link(nc.vector.tensor_tensor(r, a, parts[:, c, :], ALU.subtract))
                link(nc.vector.tensor_copy(parts[:, c + 1, :], r))
                nc.vector.tensor_tensor(parts[:, c + 2, :], r, parts[:, c + 1, :],
                                        ALU.subtract).then_inc(split_ready, 1)

            def normalise(u):
                b, g = divmod(u, UB)
                dve.wait_ge(p1_full, p1("ott", u) + 1)
                v = p1_bank[:, :].rearrange("p (t j c) -> p t j c", t=TB, c=VC)
                link(nc.vector.reciprocal(rc[:, :, :], v[:, :, :, D]))
                if g == 0 and b > 0:
                    dve.wait_ge(p0_full, p0("attnt", b - 1) + 1)
                nc.vector.tensor_tensor(
                    attn[:, :, g * HU * D:(g + 1) * HU * D].rearrange("p t (j d) -> p t j d", d=D),
                    v[:, :, :, 0:D], rc[:, :, :].unsqueeze(3).broadcast_to([P, TB, HU, D]),
                    ALU.mult).then_inc(norm_done, 1)
                dve.wait_ge(norm_done, u + 1)
                dve.sem_inc(p1_read, 1)

            def residual(b):
                dve.wait_ge(p1_full, p1("wo", b) + 1)
                xs = x[:, b * TB:(b + 1) * TB, :]
                nc.vector.tensor_tensor(xs, xs, p1_bank[:, :].rearrange("p (t e) -> p t e", e=E),
                                        ALU.add).then_inc(p1_read, 1)
                dve.wait_ge(p1_read, p1("wo", b) + 1)
                ln_stats(b, 1)

            def route(b):
                dve.wait_ge(p1_full, p1("logits", b) + 1)
                dve.wait_ge(c_loaded, 48)
                nc.vector.tensor_copy(lg[:, :, :], p1_bank[:, 0:TB * NE].rearrange("p (t e) -> p t e", e=NE)
                                      ).then_inc(p1_read, 1)
                dve.wait_ge(p1_read, p1("logits", b) + 1)
                if b > 0:
                    dve.wait_ge(tanh_ready, b)
                nc.vector.tensor_reduce(mx4[:, :], lg[:, :, :], AX.X, ALU.max).then_inc(mx4_ready, 1)
                dve.wait_ge(mx4_ready, b + 1)
                link(nc.vector.tensor_tensor(eq[:, :, :], lg[:, :, :],
                                             mx4[:, :].unsqueeze(2).broadcast_to([P, TB, NE]), ALU.is_equal))
                link(nc.vector.tensor_tensor(eq[:, :, :], eq[:, :, :],
                                             small[:, 0:NE].unsqueeze(1).broadcast_to([P, TB, NE]), ALU.mult))
                link(nc.vector.tensor_reduce(c4[:, :], eq[:, :, :], AX.X, ALU.max))
                nc.vector.tensor_tensor(onehot[:, b * TB:(b + 1) * TB, :], eq[:, :, :],
                                        c4[:, :].unsqueeze(2).broadcast_to([P, TB, NE]),
                                        ALU.is_equal).then_inc(onehot_ready, 1)

            def expert_rows(b):
                dve.wait_ge(tanh_ready, b + 1)
                link(nc.vector.tensor_scalar(sg4[:, :], th[:, :], 0.5, 0.5, ALU.mult, ALU.add))
                if b == 0:
                    dve.wait_ge(ids_done, 1)
                nc.vector.tensor_tensor(rows[:, b * TB:(b + 1) * TB, 0:E], xn2[:, :, :],
                                        sg4[:, :].unsqueeze(2).broadcast_to([P, TB, E]),
                                        ALU.mult).then_inc(rows_ready, 1)

            nc.vector.memset(half[:, :], -0.5).then_inc(half_done, 1)
            nc.vector.memset(vaug[:, :, :, :], 0.0).then_inc(vones_done, 1)
            ln_stats(0, 0)
            ln_apply(0, 0)
            dve.wait_ge(w_loaded, 16 * 11)
            dve.wait_ge(vones_done, 1)
            nc.vector.memset(vaug[:, :, :, D], 1.0).then_inc(vones_done, 1)
            for i in range(4):
                rope(0, i)
                if i % 2:
                    split_here(i // 2)
            ln_stats(1, 0)
            ln_apply(1, 0)
            for i in range(NC):
                reduce_chunk(0, i)
            for i in range(4):
                split_maxima(0, i)
            for i in range(NC):
                reduce_chunk(1, i)
            for u in range(STEPS):
                b, g = divmod(u, UB)
                todo = extras(u)
                for i in range(NC):
                    if u + 2 < U:
                        reduce_chunk(u + 2, i)
                    if u + 1 < U and i < 4:
                        split_maxima(u + 1, i)
                    for at, name, arg in todo:
                        if min(at + 1, NC - 1) != i:
                            continue
                        if name == "proj":
                            rope(*arg)
                        elif name == "ott":
                            normalise(arg)
                        elif name == "wo":
                            residual(arg)
                        elif name == "logits":
                            route(arg)
                    if g == 1 and b > 0 and i == 2:
                        ln_apply(b - 1, 1)
                    if g == 2 and b > 0 and i == 5:
                        expert_rows(b - 1)
                    if g == 2 and b + 2 < B and i == 7:
                        ln_stats(b + 2, 0)
                    if g == 2 and b + 2 < B and i == 9:
                        ln_apply(b + 2, 0)
            expert_rows(B - 1)

            def shared_mul(b):
                for c in range(2):
                    dve.wait_ge(sh_silu, 2 * b + c + 1)
                    dve.wait_ge(sh_full, 4 * b + 2 + c + 1)
                    if b > 1:
                        dve.wait_ge(shd_full, b - 1)
                    nc.vector.tensor_tensor(shh[:, b % 2, c, :], b_bank[c][:, :], shg[:, c, :],
                                            ALU.mult).then_inc(sh_mul, 1)

            def shared_add(b):
                dve.wait_ge(shd_full, b + 1)
                xs = x[:, b * TB:(b + 1) * TB, :]
                nc.vector.tensor_tensor(xs, xs, b_bank[2][:, :].rearrange("p (t e) -> p t e", e=E),
                                        ALU.add).then_inc(base_done, 1)

            shared_mul(0)
            dve.wait_ge(rank_full, 1)
            link(nc.vector.tensor_tensor(cmp16[:, :], p0_bank[0:NE, 0:NE], small[0:NE, NE:2 * NE], ALU.is_gt))
            link(nc.vector.tensor_reduce(tsum[:, :], cmp16[:, :], AX.X, ALU.add))
            nc.vector.tensor_scalar(tsb[:, :], rankc[0:NE, P:2 * P], tsum[:, 0:1], None,
                                    ALU.mult).then_inc(tsb_ready, 1)
            dve.wait_ge(base_full, 1)
            link(nc.vector.tensor_scalar(base[:, :], p0_bank[:, 0:2 * NE], float(P), None, ALU.mult))
            link(nc.vector.tensor_tensor(rk[:, :, :], p1_bank[:, 0:T * NE].rearrange("p (t e) -> p t e", e=NE),
                                         base[:, 0:NE].unsqueeze(1).broadcast_to([P, T, NE]), ALU.add))
            link(nc.vector.tensor_tensor(rk[:, :, :], rk[:, :, :], onehot[:, :, :], ALU.mult))
            link(nc.vector.tensor_reduce(posf[:, :], rk[:, :, :], AX.X, ALU.add))
            nc.vector.tensor_copy(posi[:, :], posf[:, :]).then_inc(pos_ready, 1)
            link(nc.vector.tensor_tensor(cmpt[:, :, :], base[0:1, NE:2 * NE].unsqueeze(1).broadcast_to([1, NT, NE]),
                                         small[0:1, 4 * NE:4 * NE + NT].unsqueeze(2).broadcast_to([1, NT, NE]),
                                         ALU.is_le))
            link(nc.vector.tensor_reduce(expf[:, :], cmpt[:, :, :], AX.X, ALU.add))
            nc.vector.tensor_scalar(expi[:, :], expf[:, :], float(NE - 1), None, ALU.min).then_inc(experts_ready, 1)
            for b in range(1, B):
                shared_mul(b)
                shared_add(b - 1)
            shared_add(B - 1)

            def tile_ids(r, k):
                dve.wait_ge(xin_loaded[k % RING], 16 * (r + k // RING + 1))
                nc.vector.tensor_copy(ids[:, bass.ds(r * RING + k, 1)],
                                      xin[:, k % RING, E:ROW].bitcast(I32)).then_inc(ids_ready, 1)

            def tile_mul(r, k, fill=False):
                dve.wait_ge(silu_ready, r * RING + (k + 1))
                if not fill:
                    dve.wait_ge(ht_full, r * RING + (k - 1))
                nc.vector.tensor_tensor(hh[:, k % 2, :], a_bank[k % 2][:, F:2 * F], sg[:, k % 2, :],
                                        ALU.mult).then_inc(hh_ready, 1)

            def tile_ht(r, k, fill=False):
                dve.wait_ge(ht_full, r * RING + (k + 1))
                if not fill:
                    dve.wait_ge(y_full, r * RING + (k - 1))
                nc.vector.tensor_copy(ht[:, k % 2, :, :],
                                      b_bank[k % 2][:, 0:F].rearrange("p (c n) -> p c n", c=2)).then_inc(ht_ready, 1)

            for k in range(RING):
                tile_ids(0, k)
                if k >= 1:
                    tile_mul(0, k - 1, k - 1 < 2)
                if k >= 2:
                    tile_ht(0, k - 2, True)
            with dve.Fori(1, NT // RING) as r:
                for k in range(RING):
                    tile_ids(r, k)
                    tile_mul(r, k - 1)
                    tile_ht(r, k - 2)
            end = NT // RING
            tile_mul(end, -1)
            tile_ht(end, -2)
            tile_ht(end, -1)
            for b in range(B):
                dve.wait_ge(yl_loaded[b], 16)
                xs = x[:, b * TB:(b + 1) * TB, :]
                nc.vector.tensor_tensor(xs, xs, yl[:, b * TB:(b + 1) * TB, :], ALU.add).then_inc(final_ready, 1)

        @block.gpsimd
        def _(pool):
            step = [0]
            ln = [0]

            def root():
                k = ln[0]
                ln[0] += 1
                pool.wait_ge(half_done, 1)
                pool.wait_ge(var_ready, k + 1)
                nc.gpsimd.tensor_tensor(rstd[:, k % 2, :], var[:, k % 2, :], half[:, :], ALU.pow).then_inc(rstd_ready, 1)

            def split(n, qk, i):
                a, r = t1[:, qk, :], t2[:, qk, :]
                c = 3 * qk
                if i == 0:
                    pool.wait_ge(p1_read, p1("proj", (n, 2 * qk + 1)) + 1)
                else:
                    pool.wait_ge(split_step, step[0])
                if i == 0:
                    ins = nc.gpsimd.tensor_tensor(a, a, r, ALU.add)
                elif i == 1:
                    pool.wait_ge(parts_sent, 96 * n)
                    ins = nc.gpsimd.tensor_copy(parts[:, c, :], a)
                elif i == 2:
                    ins = nc.gpsimd.tensor_tensor(r, a, parts[:, c, :], ALU.subtract)
                elif i == 3:
                    ins = nc.gpsimd.tensor_copy(parts[:, c + 1, :], r)
                else:
                    nc.gpsimd.tensor_tensor(parts[:, c + 2, :], r, parts[:, c + 1, :],
                                            ALU.subtract).then_inc(split_ready, 1)
                    return
                ins.then_inc(split_step, 1)
                step[0] += 1

            def select(u, kt):
                w, off = S - kt * P, PT_OFF[kt]
                pool.wait_ge(b_read, NC * u + LAST_CHUNK[kt] + 1)
                v = pt[:, u % 2, off:off + HU * w].rearrange("p (j w) -> p j w", j=HU)[:, :, 0:P]
                nc.gpsimd.affine_select(out=v, in_=v, pattern=[[0, HU], [1, P]], compare_op=ALU.is_ge,
                                        fill=fill, base=0, channel_multiplier=-1).then_inc(masked, 1)

            fill = pool.to_reg(0.0)
            nc.gpsimd.memset(kst[32:64, :, :].bitcast(I32), 0).then_inc(zeros_done, 1)
            pool.wait_ge(zeros_done, 1)
            root()
            pool.wait_ge(rstd_ready, 1)
            nc.gpsimd.memset(qst[32:64, :, :].bitcast(I32), 0).then_inc(zeros_done, 1)
            pool.wait_ge(zeros_done, 2)
            root()
            nc.gpsimd.iota(rows[:, :, E:ROW].bitcast(I32), [[P, T]], base=0, channel_multiplier=1).then_inc(ids_done, 1)
            nc.gpsimd.memset(zrow[:, 0:E], 0.0).then_inc(zrow_done, 1)
            nc.gpsimd.memset(zrow[:, E:ROW].bitcast(I32), NOBODY).then_inc(zrow_done, 1)
            for u in range(U):
                b, g = divmod(u, UB)
                if g == 1 and b > 0:
                    root()
                if g == 1 and b + 1 < B:
                    split(b + 1, 1, 0)
                    split(b + 1, 1, 1)
                select(u, 0)
                if b + 1 < B and g < 2:
                    for i in range(3) if g == 0 else range(2, 5):
                        split(b + 1, g, i)
                select(u, 1)
                if b + 1 < B and g == 0:
                    for i in range(3, 5):
                        split(b + 1, 0, i)
                select(u, 2)
                if g == 2 and b + 2 < B:
                    root()
                select(u, 3)
            root()
            bound = pool.to_reg(NT * P - 1)
            token_bound = pool.to_reg(B * S - 1)
            pool.wait_ge(table_cleared, 16)
            pool.wait_ge(rows_ready, B)
            pool.wait_ge(pos_ready, 1)
            for t in range(T):
                nc.gpsimd.indirect_dma_start(rows_scr.ap(), bass.IndirectOffsetOnAxis(ap=posi[:, t:t + 1], axis=0),
                                             rows[:, t, :], None, bounds_check=bound,
                                             oob_is_err=False).then_inc(scattered, 16)
            for i in range(NT):
                pool.wait_ge(ids_ready, i + 1)
                pool.wait_ge(y_ready, i + 1)
                nc.gpsimd.indirect_dma_start(y_scr.ap(), bass.IndirectOffsetOnAxis(ap=ids[:, i:i + 1], axis=0),
                                             yt[:, i % RING, :], None, bounds_check=token_bound,
                                             oob_is_err=False).then_inc(y_sent[i % RING], 16)


def constants():
    import numpy as np
    f4, bf = np.float32, mybir.dt.np(BF16)
    inv = (1.0 / (f4(10000.0) ** (np.arange(0, D, 2, dtype=f4) / f4(D)))).astype(f4)
    freqs = np.outer(np.arange(S, dtype=f4), inv).astype(f4)
    emb = np.concatenate([freqs, freqs], -1)
    sign = np.where(np.arange(D) % 2 == 0, -1.0, 1.0).astype(f4)
    cos = np.repeat(np.cos(emb).T.astype(f4), H, axis=0)
    sin = np.repeat((np.sin(emb) * sign).T.astype(f4), H, axis=0)
    i = np.arange(P)
    mask = np.where(i[None, :] > i[:, None], -1e30, 0.0)
    mask = np.repeat(mask[:, None, :], HU, axis=1).astype(bf)
    sel = np.zeros((3, HU, UB, HU, S))
    for j in range(HU):
        sel[:, j, :, j, :] = 1.0
    sel = sel.reshape(3 * HU, H, S).astype(bf)
    rank = np.zeros((P, 3 * P))
    rank[:, 0:P] = i[:, None] < i[None, :]
    rank[:, P:2 * P] = 1.0
    e = np.arange(NE)
    rank[0:NE, 2 * P:2 * P + NE] = e[:, None] < e[None, :]
    rank[0:NE, 2 * P + NE:2 * P + 2 * NE] = e[:, None] <= e[None, :]
    small = np.zeros((P, 4 * NE + 2 * NT), f4)
    small[:, 0:NE] = NE - e
    small[:, NE:2 * NE] = P * e
    small[:, 4 * NE:4 * NE + NT] = P * np.arange(NT)
    return {
        "cos": cos, "sin": sin, "ident": np.eye(P, dtype=f4), "identb": np.eye(P).astype(bf),
        "mask": mask, "sel": sel, "rank": rank.astype(bf), "small": small,
    }


def kernel(L0_attn_x, L0_attn_Wq, L0_attn_Wk, L0_attn_Wv, L0_attn_Wo, L0_ffn_w_router, L0_ffn_gate_up_proj,
           L0_ffn_down_proj, L0_ffn_w_gate, L0_ffn_w_up, L0_ffn_w_down):
    import numpy as np
    import concourse.bacc as bacc
    from concourse.bass_utils import run_bass_kernel_spmd

    d_h = np.arange(H * D).reshape(H, D).T.reshape(-1)
    swapped = (np.arange(H * D) ^ 1).reshape(H, D).T.reshape(-1)
    wq, wk = np.asarray(L0_attn_Wq), np.asarray(L0_attn_Wk)
    c = constants()
    arrays = {
        "x": np.asarray(L0_attn_x),
        "wq": wq[d_h].T, "wqs": wq[swapped].T, "wk": wk[d_h].T, "wks": wk[swapped].T,
        "wv": np.asarray(L0_attn_Wv).T, "wo": np.asarray(L0_attn_Wo).T,
        "w_router": np.asarray(L0_ffn_w_router).T,
        "w_gu": np.asarray(L0_ffn_gate_up_proj), "w_dn": np.asarray(L0_ffn_down_proj),
        "w_sh": np.concatenate([np.asarray(L0_ffn_w_gate).T, np.asarray(L0_ffn_w_up).T], axis=1),
        "w_shd": np.asarray(L0_ffn_w_down).T,
        **c,
    }
    arrays = {"in_" + k: np.ascontiguousarray(v) for k, v in arrays.items()}
    nc = bacc.Bacc("TRN2", target_bir_lowering=False, num_devices=1)
    args = [nc.dram_tensor(k, v.shape, mybir.dt.from_np(v.dtype), kind="ExternalInput").ap()
            for k, v in arrays.items()]
    out = nc.dram_tensor("out", (B, S, E), F32, kind="ExternalOutput").ap()
    block_kernel(nc, *args, out)
    result = run_bass_kernel_spmd(nc, [arrays], core_ids=[0])
    return result.results[0]["out"]
```

```python
from contextlib import ExitStack

import concourse.bass as bass
from concourse import mybir

F32 = mybir.dt.float32
BF16 = mybir.dt.bfloat16
I32 = mybir.dt.int32
ALU = mybir.AluOpType
ACT = mybir.ActivationFunctionType
AX = mybir.AxisListType

P = 128
B, S, E = 4, 512, 128
H, D = 16, 8
NE, F = 16, 256
T = B * S // P
TB = S // P
HU = 4
UB = H // HU
U = B * UB
SCALE = float(D) ** -0.5
EPS = 1e-5
PARTS = 6
KS = PARTS * D
MROW = 64
KM = MROW + 3 * HU
VC = 32
NT = B * S // P + NE
ROW = E + 1
NOBODY = 1 << 20
RING = 4

CHUNKS = [(3, h, 1) for h in range(4)] + [(2, h, 1) for h in range(4)] + [(1, 0, 2), (1, 2, 2), (0, 0, 4)]
NC = len(CHUNKS)
PT_OFF = [0, HU * 512, HU * (512 + 384), HU * (512 + 384 + 256)]
PT_LEN = HU * (512 + 384 + 256 + 128)
LAST_CHUNK = [3, 7, 9, 10]


def width(block):
    return P * (block + 1)


def extras(u):
    b, g = divmod(u, UB)
    out = []
    if 0 < u <= U:
        out += [(1, "pv", (u - 1, 2)), (2, "pv", (u - 1, 3)), (4 if u % UB in (0, 3) else 5, "ott", u - 1)]
    if g == 0 and 0 < b < B:
        out += [(3, "v", b)]
    if u + 1 < U:
        out += [(4, "mt", u + 1)]
    if u < U:
        out += [(6, "pv", (u, 0)), (10, "pv", (u, 1))]
    if g == 2 and b + 2 < B:
        out += [(8, "xn1t", b + 2)]
    if g == 3 and b + 2 < B:
        out += [(at, "proj", (b + 2, i)) for i, at in enumerate((0, 2, 6, 8))]
    if g == 0 and b > 0:
        out += [(8, "attnt", b - 1), (10, "wo", b - 1)]
    if g == 1 and b > 0:
        out += [(7, "xn2t", b - 1), (9, "logits", b - 1)]
    return sorted(out, key=lambda x: x[0])


STEPS = U + 2
PROLOGUE = [("xn1t", 0), ("proj0", 0), ("xn1t", 1), ("v", 0)] + [("proj", (1, i)) for i in range(4)] + [("mt", 0)]
ORDER = PROLOGUE + [(t, a) for u in range(STEPS) for _, t, a in extras(u)]
P0_USES = [x for x in ORDER if x[0] in ("xn1t", "v", "mt", "attnt", "xn2t")]
P1_USES = [x for x in ORDER if x[0] in ("proj", "ott", "wo", "logits")]


def p0(task, arg):
    return P0_USES.index((task, arg))


def p1(task, arg):
    return P1_USES.index((task, arg))


def block_kernel(nc, x_in, w_att_in, w_router, w_gu, w_dn, w_sh, w_shd, rot_in, ident_in, ident_mask_in,
                 sel_in, rank_in, small_in, out):
    q_scr = nc.dram_tensor("q_scr", [2, KS, H, S], BF16)
    k_scr = nc.dram_tensor("k_scr", [2, KS, H, S], BF16)
    rows_scr = nc.dram_tensor("rows_scr", [NT * P, ROW], F32)
    y_scr = nc.dram_tensor("y_scr", [B * S, E], F32)
    x_dram = x_in.rearrange("b (t p) d -> b p t d", p=P)
    out_dram = out.rearrange("b (t p) d -> b p t d", p=P)

    with ExitStack() as ctx:
        def sb(name, shape, dt=F32):
            return ctx.enter_context(nc.sbuf_tensor(name, shape, dt))

        def sem(name):
            return ctx.enter_context(nc.semaphore(name))

        def bank(name):
            return ctx.enter_context(nc.psum_tensor(name, [P, 512], F32))

        x = sb("x", [P, T, E])
        qst = sb("qst", [P, H, S], BF16)
        kst = sb("kst", [P, H, S], BF16)
        pt = sb("pt", [P, 2, PT_LEN])
        wgu_sb = sb("wgu_sb", [P, NE, 2 * F])
        wdn_sb = sb("wdn_sb", [P, NE, 2, E])
        vaug = sb("vaug", [P, TB, H, VC])
        xn2t = sb("xn2t", [P, B * S])
        rows = sb("rows", [P, T, ROW])
        xnt = sb("xnt", [P, 2, S])
        xn1 = sb("xn1", [P, TB, E])
        xn2 = sb("xn2", [P, TB, E])
        rot_sb = sb("rot_sb", [P, 2, S])
        t1 = sb("t1", [P, 2, S])
        t2 = sb("t2", [P, 2, S])
        parts = sb("parts", [P, 6, S], BF16)
        ots = sb("ots", [P, S])
        attn = sb("attn", [P, TB, H * D])
        attnt = sb("attnt", [P, S])
        w_att = sb("w_att", [P, 6, E])
        wr_sb = sb("wr_sb", [P, NE])
        wsh_sb = sb("wsh_sb", [P, 2 * F])
        wshd_sb = sb("wshd_sb", [P, 2, E])
        ident = sb("ident", [P, P])
        ident_mask = sb("ident_mask", [P, 1 + HU, P], BF16)
        identb, mask = ident_mask[:, 0, :], ident_mask[:, 1:1 + HU, :]
        rankc = sb("rankc", [P, 3 * P], BF16)
        small = sb("small", [P, 4 * NE + 2 * NT])
        mx = sb("mx", [P, 2, TB, HU])
        mres = sb("mres", [P, TB, HU])
        mparts = sb("mparts", [P, TB, 3, HU], BF16)
        m12 = sb("m12", [3 * HU, S], BF16)
        stats = sb("stats", [P, TB, 6])
        mv = sb("mv", [P, 2, TB, 2])
        var = sb("var", [P, 2, TB])
        rstd = sb("rstd", [P, 2, TB])
        half = sb("half", [P, TB])
        rc = sb("rc", [P, TB, HU])
        lg = sb("lg", [P, TB, NE])
        eq = sb("eq", [P, TB, NE])
        mx4 = sb("mx4", [P, TB])
        c4 = sb("c4", [P, TB])
        th = sb("th", [P, TB])
        sg4 = sb("sg4", [P, TB])
        onehot = sb("onehot", [P, T, NE], BF16)
        zrow = sb("zrow", [P, ROW])
        cmp16 = sb("cmp16", [NE, NE])
        tsum = sb("tsum", [NE, 1])
        tsb = sb("tsb", [NE, P], BF16)
        base = sb("base", [P, 2 * NE])
        cmpt = sb("cmpt", [1, NT, NE])
        expf = sb("expf", [1, NT])
        expi = sb("expi", [1, NT], I32)
        rk = sb("rk", [P, T, NE])
        posf = sb("posf", [P, T])
        posi = sb("posi", [P, T], I32)
        ids = sb("ids", [P, NT], I32)
        shg = pt[:, 0, 0:1024].rearrange("p (c n) -> p c n", c=2)
        shh = pt[:, 0, 1024:3072].rearrange("p (r c n) -> p r c n", r=2, c=2)
        xt = pt[:, 0, 3072:3328].rearrange("p (r n) -> p r n", r=2)
        sg = pt[:, 0, 3328:3840].rearrange("p (r n) -> p r n", r=2)
        hh = pt[:, 0, 3840:4352].rearrange("p (r n) -> p r n", r=2)
        ht = pt[:, 0, 4352:4864].rearrange("p (r c n) -> p r c n", r=2, c=2)
        yl = pt[:, 1, 0:2048].rearrange("p (t d) -> p t d", t=T)
        yt = pt[:, 1, 2048:2560].rearrange("p (r n) -> p r n", r=RING)
        xin = pt[:, 1, 2560:2560 + RING * ROW].rearrange("p (r n) -> p r n", r=RING)

        a_bank = [bank("a0"), bank("a1")]
        b_bank = [bank("b0"), bank("b1"), bank("b2")]
        ot_bank = bank("ot")
        p0_bank = bank("p0")
        p1_bank = bank("p1")
        proj0_bank = a_bank + b_bank[0:2]
        mt_view = p0_bank[0:3 * HU, 0:S // 2].bitcast(BF16)

        x_in_sem = [sem(f"x_loaded{b}") for b in range(B)]
        ident_loaded = sem("ident_loaded")
        w_loaded = sem("w_loaded")
        rot_loaded = sem("rot_loaded")
        mask_loaded = sem("mask_loaded")
        proj0_full = sem("proj0_full")
        proj0_read = sem("proj0_read")
        c_loaded = sem("c_loaded")
        wexp_loaded = sem("wexp_loaded")
        sel_loaded = sem("sel_loaded")
        zeros_done = sem("zeros_done")
        vones_done = sem("vones_done")
        half_done = sem("half_done")
        zrow_done = sem("zrow_done")
        table_cleared = sem("table_cleared")
        ids_done = sem("ids_done")
        var_ready = sem("var_ready")
        rstd_ready = sem("rstd_ready")
        xn1_ready = sem("xn1_ready")
        xn2_ready = sem("xn2_ready")
        p0_full = sem("p0_full")
        p0_read = sem("p0_read")
        p1_full = sem("p1_full")
        p1_read = sem("p1_read")
        rope_ready = sem("rope_ready")
        split_ready = sem("split_ready")
        split_step = sem("split_step")
        parts_sent = sem("parts_sent")
        slot_loaded = [sem(f"slot_loaded{g}") for g in range(UB)]
        a_full = sem("a_full")
        a_read = sem("a_read")
        b_full = sem("b_full")
        b_read = sem("b_read")
        masked = sem("masked")
        pv_done = sem("pv_done")
        ot_read = sem("ot_read")
        mparts_ready = sem("mparts_ready")
        mrow_loaded = [sem("mrow_loaded0"), sem("mrow_loaded1")]
        norm_done = sem("norm_done")
        tanh_ready = sem("tanh_ready")
        mx4_ready = sem("mx4_ready")
        rows_ready = sem("rows_ready")
        onehot_ready = sem("onehot_ready")
        rank_full = sem("rank_full")
        tsb_ready = sem("tsb_ready")
        base_full = sem("base_full")
        experts_ready = sem("experts_ready")
        pos_ready = sem("pos_ready")
        scattered = sem("scattered")
        sh_full = sem("sh_full")
        sh_silu = sem("sh_silu")
        sh_mul = sem("sh_mul")
        shd_full = sem("shd_full")
        base_done = sem("base_done")
        xin_loaded = [sem(f"xin_loaded{i}") for i in range(RING)]
        xt_full = sem("xt_full")
        xt_ready = sem("xt_ready")
        ids_ready = sem("ids_ready")
        h_full = sem("h_full")
        silu_ready = sem("silu_ready")
        hh_ready = sem("hh_ready")
        ht_full = sem("ht_full")
        ht_ready = sem("ht_ready")
        y_full = sem("y_full")
        y_ready = sem("y_ready")
        y_sent = [sem(f"y_sent{i}") for i in range(RING)]
        yl_loaded = [sem(f"yl_loaded{b}") for b in range(B)]
        final_ready = sem("final_ready")
        stored = sem("stored")
        v_chain = sem("v_chain")
        v_copied = sem("v_copied")

        block = ctx.enter_context(nc.Block())

        @block.sync
        def _(sp):
            for b in range(B):
                sp.dma_start(x[:, b * TB:(b + 1) * TB, :], x_dram[b]).then_inc(x_in_sem[b], 16)
                if b == 0:
                    sp.dma_start(ident[:], ident_in).then_inc(ident_loaded, 16)
                if b == 1:
                    sp.dma_start(w_att[:], w_att_in).then_inc(w_loaded, 16)
                    sp.dma_start(rot_sb[:], rot_in).then_inc(rot_loaded, 16)
                    sp.dma_start(ident_mask[:], ident_mask_in).then_inc(mask_loaded, 16)
            sp.wait_ge(zeros_done, 2)
            sp.dma_start(kst[MROW:KM, :, :], sel_in).then_inc(sel_loaded, 16)

            def send_parts(n):
                par = n % 2
                sp.wait_ge(split_ready, 2 * n + 1)
                q_to = q_scr.ap()[par].rearrange("(r d) h t -> (d h) r t", d=D)
                k_to = k_scr.ap()[par].rearrange("(r d) h t -> (d h) r t", d=D)
                for to, r0, c, rep in ((q_to, 0, 0, 3), (q_to, 3, 1, 2), (q_to, 5, 2, 1)):
                    sp.dma_start(to[:, r0:r0 + rep, :],
                                 parts[:, c:c + 1, :].broadcast_to([P, rep, S])).then_inc(parts_sent, 16)
                sp.wait_ge(split_ready, 2 * n + 2)
                for to, r0, c, n_c in ((k_to, 0, 3, 3), (k_to, 3, 3, 2), (k_to, 5, 3, 1)):
                    sp.dma_start(to[:, r0:r0 + n_c, :], parts[:, c:c + n_c, :]).then_inc(parts_sent, 16)
                sp.wait_ge(parts_sent, 96 * (n + 1))

            def load_slot(n, g):
                if n > 0:
                    sp.wait_ge(b_full, NC * (UB * (n - 1) + g + 1))
                hs = slice(HU * g, HU * g + HU)
                sp.dma_start(qst[0:KS, hs, :], q_scr.ap()[n % 2, :, hs, :]).then_inc(slot_loaded[g], 16)
                sp.dma_start(kst[0:KS, hs, :], k_scr.ap()[n % 2, :, hs, :]).then_inc(slot_loaded[g], 16)

            def load_maxima(u):
                g = u % UB
                sp.wait_ge(p0_read, p0("mt", u) + 1)
                if u >= UB:
                    sp.wait_ge(b_full, NC * (u - UB + 1))
                sp.dma_start(qst[MROW:KM, HU * g:HU * g + HU, :],
                             m12[:, :].rearrange("p (o s) -> p o s", o=1).broadcast_to([3 * HU, HU, S])
                             ).then_inc(mrow_loaded[u % 2], 16)

            send_parts(0)
            for g in range(UB):
                load_slot(0, g)
            sp.dma_start(wr_sb[:], w_router).then_inc(c_loaded, 16)
            sp.dma_start(rankc[:], rank_in).then_inc(c_loaded, 16)
            sp.dma_start(small[:], small_in).then_inc(c_loaded, 16)
            load_maxima(0)
            sp.wait_ge(zrow_done, 2)
            sp.dma_start(rows_scr.ap().rearrange("(t p) c -> p t c", p=P),
                         zrow[:, :].rearrange("p (o c) -> p o c", o=1).broadcast_to([P, NT, ROW])
                         ).then_inc(table_cleared, 16)
            for u in range(U):
                b, g = divmod(u, UB)
                if g > 0 and b + 1 < B:
                    load_slot(b + 1, g - 1)
                if g == 0 and b > 0:
                    load_slot(b, UB - 1)
                if u + 1 < U:
                    load_maxima(u + 1)
                if g == 0 and b + 1 < B:
                    send_parts(b + 1)
                sp.dma_start(wgu_sb[:, u, :], w_gu[u]).then_inc(wexp_loaded, 16)
                sp.dma_start(wdn_sb[:, u, :, :], w_dn[u].rearrange("(c p) h -> p c h", p=P)).then_inc(wexp_loaded, 16)
            sp.dma_start(wsh_sb[:], w_sh).then_inc(wexp_loaded, 16)
            sp.dma_start(wshd_sb[:], w_shd.rearrange("(c p) h -> p c h", p=P)).then_inc(wexp_loaded, 16)

            sp.wait_ge(scattered, 16 * T)

            def load_rows(r, k, first):
                if not first:
                    sp.wait_ge(xt_full, r * RING + (k - RING + 1))
                    sp.wait_ge(ids_ready, r * RING + (k - RING + 1))
                sp.dma_start(xin[:, k, :], rows_scr.ap()[bass.ds(r * (RING * P) + k * P, P), :]
                             ).then_inc(xin_loaded[k], 16)

            for k in range(RING):
                load_rows(0, k, True)
            with sp.Fori(1, NT // RING) as r:
                for k in range(RING):
                    load_rows(r, k, False)

            for k in range(RING):
                sp.wait_ge(y_sent[k], 16 * (NT // RING))
            for b in range(B):
                sp.dma_start(yl[:, b * TB:(b + 1) * TB, :],
                             y_scr.ap().rearrange("(b t p) d -> b p t d", b=B, p=P)[b]).then_inc(yl_loaded[b], 16)
            for b in range(B):
                sp.wait_ge(final_ready, b + 1)
                sp.dma_start(out_dram[b], x[:, b * TB:(b + 1) * TB, :]).then_inc(stored, 16)
            sp.wait_ge(stored, 16 * B)

        @block.tensor
        def _(pe):
            def a_chunk(u, i):
                block_, h0, n = CHUNKS[i]
                w, g, c = width(block_), u % UB, NC * u + i
                if i == 0:
                    pe.wait_ge(slot_loaded[g], 32 * (u // UB + 1))
                if c >= 2:
                    pe.wait_ge(a_read, c - 1)
                to = a_bank[c % 2]
                for j in range(n):
                    h = HU * g + h0 + j
                    pe.matmul(to[:, j * w:(j + 1) * w], qst[0:KS, h, block_ * P:(block_ + 1) * P],
                              kst[0:KS, h, 0:w], start=(j == 0), stop=False, skip_group_check=True)
                diag = to[:, 0:n * w].rearrange("p (j w) -> p j w", j=n)[:, :, w - P:w]
                pe.matmul(diag, identb, mask[:, 0:n, :], start=False, stop=True,
                          skip_group_check=True).then_inc(a_full, 1)

            def b_chunk(u, i):
                block_, h0, n = CHUNKS[i]
                w, g, c, kt = width(block_), u % UB, NC * u + i, 3 - block_
                if i == 0:
                    pe.wait_ge(mrow_loaded[u % 2], 16 * (u // 2 + 1))
                    if u < 1:
                        pe.wait_ge(sel_loaded, 16)
                if c >= 3:
                    pe.wait_ge(b_read, c - 2)
                to = b_bank[c % 3]
                for j in range(n):
                    h = HU * g + h0 + j
                    mm = pe.matmul(to[:, j * w:(j + 1) * w], kst[0:KM, h, kt * P:(kt + 1) * P],
                                   qst[0:KM, h, kt * P:S], start=True, stop=True)
                mm.then_inc(b_full, 1)

            def transposes(to, src):
                for t in range(TB):
                    mm = pe.transpose(to[:, t * P:(t + 1) * P], src[:, t, :], ident[:, :])
                return mm

            def task(name, arg):
                if (name, arg) in P0_USES:
                    if p0(name, arg) > 0:
                        pe.wait_ge(p0_read, p0(name, arg))
                if (name, arg) in P1_USES:
                    if p1(name, arg) > 0:
                        pe.wait_ge(p1_read, p1(name, arg))
                if name == "xn1t":
                    pe.wait_ge(xn1_ready, arg + 1)
                    transposes(p0_bank, xn1).then_inc(p0_full, 1)
                elif name == "proj0":
                    pe.wait_ge(p0_read, p0("xn1t", 0) + 1)
                    pe.wait_ge(w_loaded, 16)
                    for i in range(4):
                        pe.matmul(proj0_bank[i][:, :], w_att[:, i, :], xnt[:, 0, :], start=True,
                                  stop=True).then_inc(proj0_full, 1)
                elif name == "proj":
                    n, i = arg
                    pe.wait_ge(p0_read, p0("xn1t", n) + 1)
                    pe.matmul(p1_bank[:, :], w_att[:, i, :], xnt[:, n % 2, :], start=True,
                              stop=True).then_inc(p1_full, 1)
                elif name == "v":
                    for t in range(TB):
                        mm = pe.matmul(p0_bank[:, t * P:(t + 1) * P], xnt[:, arg % 2, t * P:(t + 1) * P],
                                       w_att[:, 4, :], start=True, stop=True)
                    mm.then_inc(p0_full, 1)
                elif name == "mt":
                    pe.wait_ge(mparts_ready, arg + 1)
                    for t in range(TB):
                        mm = pe.transpose(mt_view[:, t * P:(t + 1) * P],
                                          mparts[:, t, :, :].rearrange("p c h -> p (c h)"), identb)
                    mm.then_inc(p0_full, 1)
                elif name == "pv":
                    u, kt = arg
                    g, w, off = u % UB, S - kt * P, PT_OFF[kt]
                    pe.wait_ge(masked, TB * u + kt + 1)
                    if kt == 0:
                        pe.wait_ge(v_copied, u // UB + 1)
                        if u > 0:
                            pe.wait_ge(ot_read, u)
                    for j in range(HU):
                        mm = pe.matmul(ot_bank[32 * j:32 * j + VC, kt * P:S], vaug[:, kt, HU * g + j, :],
                                       pt[:, u % 2, off + j * w:off + (j + 1) * w],
                                       start=(kt == 0), stop=(kt == TB - 1), tile_position=(0, 32 * j))
                    mm.then_inc(pv_done, 1)
                elif name == "ott":
                    pe.wait_ge(ot_read, arg + 1)
                    transposes(p1_bank, ots[:, :].rearrange("p (t q) -> p t q", t=TB)).then_inc(p1_full, 1)
                elif name == "attnt":
                    pe.wait_ge(norm_done, UB * (arg + 1))
                    transposes(p0_bank, attn).then_inc(p0_full, 1)
                elif name == "wo":
                    pe.wait_ge(p0_read, p0("attnt", arg) + 1)
                    for t in range(TB):
                        mm = pe.matmul(p1_bank[:, t * P:(t + 1) * P], attnt[:, t * P:(t + 1) * P],
                                       w_att[:, 5, :], start=True, stop=True)
                    mm.then_inc(p1_full, 1)
                elif name == "xn2t":
                    pe.wait_ge(xn2_ready, arg + 1)
                    transposes(p0_bank, xn2).then_inc(p0_full, 1)
                elif name == "logits":
                    pe.wait_ge(p0_read, p0("xn2t", arg) + 1)
                    pe.wait_ge(c_loaded, 48)
                    for t in range(TB):
                        c = arg * TB + t
                        mm = pe.matmul(p1_bank[:, t * NE:(t + 1) * NE], xn2t[:, c * P:(c + 1) * P],
                                       wr_sb[:, :], start=True, stop=True)
                    mm.then_inc(p1_full, 1)

            pe.wait_ge(ident_loaded, 16)
            for name, arg in PROLOGUE:
                if name == "mt":
                    pe.wait_ge(proj0_read, 4)
                    pe.wait_ge(mask_loaded, 16)
                    for i in range(NC):
                        a_chunk(0, i)
                    task(name, arg)
                    for i in range(NC):
                        a_chunk(1, i)
                else:
                    task(name, arg)
            for u in range(STEPS):
                todo = extras(u)
                for i in range(NC):
                    if u < U:
                        b_chunk(u, i)
                    if u + 2 < U:
                        a_chunk(u + 2, i)
                    for after, name, arg in todo:
                        if after == i:
                            task(name, arg)

            def shared_up(b):
                if b == 0:
                    pe.wait_ge(wexp_loaded, 32 * U + 32)
                for c in range(2):
                    if b > 0:
                        pe.wait_ge(sh_silu, 2 * (b - 1) + c + 1)
                    pe.matmul(a_bank[c][:, :], wsh_sb[:, c * P:(c + 1) * P], xn2t[:, b * S:(b + 1) * S],
                              start=True, stop=True).then_inc(sh_full, 1)
                for c in range(2):
                    if b > 0:
                        pe.wait_ge(sh_mul, 2 * (b - 1) + c + 1)
                    pe.matmul(b_bank[c][:, :], wsh_sb[:, F + c * P:F + (c + 1) * P],
                              xn2t[:, b * S:(b + 1) * S], start=True, stop=True).then_inc(sh_full, 1)

            def shared_down(b):
                pe.wait_ge(sh_mul, 2 * b + 2)
                if b > 0:
                    pe.wait_ge(base_done, b)
                for t in range(TB):
                    for c in range(2):
                        mm = pe.matmul(b_bank[2][:, t * P:(t + 1) * P], shh[:, b % 2, c, t * P:(t + 1) * P],
                                       wshd_sb[:, c, :], start=(c == 0), stop=(c == 1))
                mm.then_inc(shd_full, 1)

            def ranks():
                pe.wait_ge(onehot_ready, B)
                pe.wait_ge(p0_read, len(P0_USES))
                pe.wait_ge(p1_read, len(P1_USES))
                r = p1_bank[:, 0:T * NE].rearrange("p (t e) -> p t e", e=NE)
                pe.matmul(r, rankc[:, 0:P], onehot[:, :, :], start=True, stop=False, skip_group_check=True)
                for t in range(T - 1):
                    pe.matmul(r[:, t + 1:T, :], rankc[:, P:2 * P],
                              onehot[:, t:t + 1, :].broadcast_to([P, T - 1 - t, NE]),
                              start=False, stop=(t == T - 2), skip_group_check=True)
                for t in range(T):
                    mm = pe.matmul(p0_bank[0:NE, 0:NE], onehot[:, t, :], rankc[:, P:P + NE],
                                   start=(t == 0), stop=(t == T - 1))
                mm.then_inc(rank_full, 1)
                pe.wait_ge(tsb_ready, 1)
                pe.matmul(p0_bank[:, 0:2 * NE], tsb[:, :], rankc[0:NE, 2 * P:2 * P + 2 * NE],
                          start=True, stop=True).then_inc(base_full, 1)

            shared_up(0)
            ranks()
            for b in range(1, B):
                shared_up(b)
                shared_down(b - 1)
            shared_down(B - 1)

            x_bank, h_bank, ht_bank, y_bank = [p0_bank, p1_bank], a_bank, b_bank[0:2], [b_bank[2], ot_bank]

            expert_reg = [pe.alloc_register(f"expert{i}") for i in range(4)]

            def load_expert(r, k):
                pe.reg_load(expert_reg[k % 4], expi[0:1, bass.ds(r * RING + k, 1)])

            def expert_of(k):
                return pe.snap(expert_reg[k % 4], min_val=0, max_val=NE - 1)

            def tile_transpose(r, k, fill=False):
                pe.wait_ge(xin_loaded[k % RING], 16 * (r + k // RING + 1))
                if not fill:
                    pe.wait_ge(xt_ready, r * RING + (k - 1))
                pe.transpose(x_bank[k % 2][:, 0:P], xin[:, k % RING, 0:E], ident[:, :]).then_inc(xt_full, 1)

            def tile_up(r, k, e, fill=False):
                pe.wait_ge(xt_ready, r * RING + (k + 1))
                if not fill:
                    pe.wait_ge(hh_ready, r * RING + (k - 1))
                pe.matmul(h_bank[k % 2][:, :], xt[:, k % 2, :],
                          wgu_sb[:, bass.ds(e, 1), :].rearrange("p o f -> p (o f)"),
                          start=True, stop=True).then_inc(h_full, 1)

            def tile_hidden(r, k, fill=False):
                pe.wait_ge(hh_ready, r * RING + (k + 1))
                if not fill:
                    pe.wait_ge(ht_ready, r * RING + (k - 1))
                for c in range(2):
                    mm = pe.transpose(ht_bank[k % 2][:, c * P:(c + 1) * P], hh[:, k % 2, c * P:(c + 1) * P],
                                      ident[:, :])
                mm.then_inc(ht_full, 1)

            def tile_down(r, k, e, fill=False):
                pe.wait_ge(ht_ready, r * RING + (k + 1))
                if not fill:
                    pe.wait_ge(y_ready, r * RING + (k - 1))
                for c in range(2):
                    mm = pe.matmul(y_bank[k % 2][:, 0:E], ht[:, k % 2, c, :],
                                   wdn_sb[:, bass.ds(e, 1), c, :].rearrange("p o f -> p (o f)"),
                                   start=(c == 0), stop=(c == 1))
                mm.then_inc(y_full, 1)

            pe.wait_ge(experts_ready, 1)
            pe.wait_ge(base_done, B)
            pe.wait_ge(pos_ready, 1)

            def slot(r, k, n=2 * RING, end=False):
                if n >= 3 and not (end and k > 2):
                    tile_hidden(r, k - 3, n < 5)
                if n >= 4:
                    tile_down(r, k - 4, expert_of(k - 4), n < 6)
                if not end:
                    tile_transpose(r, k, n < 2)
                if n >= 1 and not (end and k > 0):
                    tile_up(r, k - 1, expert_of(k - 1), n < 3)
                if not end:
                    load_expert(r, k)

            for k in range(2 * RING):
                slot(0, k, k)
            with pe.Fori(2, NT // RING) as r:
                for k in range(RING):
                    slot(r, k)
            for k in range(4):
                slot(NT // RING, k, end=True)

        @block.scalar
        def _(act):
            def exp_chunk(u, i):
                block_, h0, n = CHUNKS[i]
                w, c, kt = width(block_), NC * u + i, 3 - block_
                act.wait_ge(b_full, c + 1)
                if i == 0 and u >= 2:
                    act.wait_ge(pv_done, TB * (u - 1))
                off = PT_OFF[kt] + h0 * w
                nc.scalar.activation(pt[:, u % 2, off:off + n * w], b_bank[c % 3][:, 0:n * w], ACT.Exp,
                                     scale=SCALE).then_inc(b_read, 1)

            def task(name, arg):
                if name == "pv":
                    u, kt = arg
                    if kt == TB - 1:
                        act.wait_ge(pv_done, TB * (u + 1))
                        if u > 0:
                            act.wait_ge(p1_full, p1("ott", u - 1) + 1)
                        nc.scalar.copy(ots[:, :], ot_bank[:, :]).then_inc(ot_read, 1)
                    return
                if (name, arg) not in P0_USES:
                    return
                act.wait_ge(p0_full, p0(name, arg) + 1)
                if name == "xn1t":
                    nc.scalar.copy(xnt[:, arg % 2, :], p0_bank[:, :]).then_inc(p0_read, 1)
                elif name == "v":
                    if arg > 0:
                        act.wait_ge(pv_done, TB * UB * arg)
                    act.wait_ge(vones_done, 2)
                    nc.scalar.copy(vaug[:, :, :, 0:D],
                                   p0_bank[:, :].rearrange("p (t h d) -> p t h d", t=TB, d=D)).then_inc(v_copied, 1)
                    act.wait_ge(v_copied, arg + 1)
                    act.sem_inc(p0_read, 1)
                elif name == "mt":
                    if arg > 0:
                        act.wait_ge(mrow_loaded[(arg - 1) % 2], 16 * ((arg - 1) // 2 + 1))
                    nc.scalar.copy(m12[:, :], mt_view).then_inc(p0_read, 1)
                elif name == "attnt":
                    nc.scalar.copy(attnt[:, :], p0_bank[:, :]).then_inc(p0_read, 1)
                elif name == "xn2t":
                    nc.scalar.copy(xn2t[:, arg * S:(arg + 1) * S], p0_bank[:, :]).then_inc(p0_read, 1)

            def gate(b):
                act.wait_ge(mx4_ready, b + 1)
                if b > 0:
                    act.wait_ge(rows_ready, b)
                nc.scalar.activation(th[:, :], mx4[:, :], ACT.Tanh, scale=0.5).then_inc(tanh_ready, 1)

            for name, arg in PROLOGUE:
                task(name, arg)
            for u in range(STEPS):
                b, g = divmod(u, UB)
                todo = extras(u)
                for i in range(NC):
                    if u < U:
                        exp_chunk(u, i)
                    for after, name, arg in todo:
                        if min(after + 1, NC - 1) == i:
                            task(name, arg)
                    if g == 2 and b > 0 and i == 2:
                        gate(b - 1)
            gate(B - 1)
            for b in range(B):
                for c in range(2):
                    act.wait_ge(sh_full, 4 * b + c + 1)
                    if b > 0:
                        act.wait_ge(sh_mul, 2 * (b - 1) + c + 1)
                    nc.scalar.activation(shg[:, c, :], a_bank[c][:, :], ACT.Silu).then_inc(sh_silu, 1)

            def tile_xt(r, k, fill=False):
                act.wait_ge(xt_full, r * RING + (k + 1))
                if not fill:
                    act.wait_ge(h_full, r * RING + (k - 1))
                nc.scalar.copy(xt[:, k % 2, :], [p0_bank, p1_bank][k % 2][:, 0:P]).then_inc(xt_ready, 1)

            def tile_silu(r, k, fill=False):
                act.wait_ge(h_full, r * RING + (k + 1))
                if not fill:
                    act.wait_ge(hh_ready, r * RING + (k - 1))
                nc.scalar.activation(sg[:, k % 2, :], a_bank[k % 2][:, 0:F], ACT.Silu).then_inc(silu_ready, 1)

            def tile_y(r, k, fill=False):
                act.wait_ge(y_full, r * RING + (k + 1))
                if not fill:
                    act.wait_ge(y_sent[k % RING], 16 * (r + k // RING))
                nc.scalar.copy(yt[:, k % RING, :], [b_bank[2], ot_bank][k % 2][:, 0:E]).then_inc(y_ready, 1)

            def slot(r, k, n=2 * RING, end=False):
                if n >= 2 and not (end and k > 1):
                    tile_silu(r, k - 2, n < 4)
                if n >= 4:
                    tile_y(r, k - 4, n < 4 + RING)
                if not end:
                    tile_xt(r, k, n < 2)

            for k in range(2 * RING):
                slot(0, k, k)
            with act.Fori(2, NT // RING) as r:
                for k in range(RING):
                    slot(r, k)
            for k in range(4):
                slot(NT // RING, k, end=True)

        @block.vector
        def _(dve):
            count = [0]

            def mark(ins):
                count[0] += 1
                ins.then_inc(v_chain, 1)
                return count[0]

            def after(n):
                dve.wait_ge(v_chain, n)

            def link(ins):
                after(mark(ins))

            def reduce_chunk(u, i):
                block_, h0, n = CHUNKS[i]
                w, c = width(block_), NC * u + i
                dve.wait_ge(a_full, c + 1)
                nc.vector.tensor_reduce(mx[:, u % 2, block_, h0:h0 + n],
                                        a_bank[c % 2][:, 0:n * w].rearrange("p (j w) -> p j w", j=n),
                                        AX.X, ALU.max).then_inc(a_read, 1)

            split_mark = [0]

            def split_maxima(u, i):
                m = mx[:, u % 2, :, :]
                if i > 0:
                    after(split_mark[0])
                if i == 0:
                    dve.wait_ge(a_read, NC * (u + 1))
                    if u > 0:
                        dve.wait_ge(p0_full, p0("mt", u - 1) + 1)
                    ins = nc.vector.tensor_scalar(mparts[:, :, 0, :], m, -1.0, None, ALU.mult)
                elif i == 1:
                    ins = nc.vector.scalar_tensor_tensor(out=mres[:, :, :], in0=m, scalar=-1.0,
                                                         in1=mparts[:, :, 0, :], op0=ALU.mult, op1=ALU.subtract)
                elif i == 2:
                    ins = nc.vector.tensor_copy(mparts[:, :, 1, :], mres[:, :, :])
                else:
                    nc.vector.tensor_tensor(mparts[:, :, 2, :], mres[:, :, :], mparts[:, :, 1, :],
                                            ALU.subtract).then_inc(mparts_ready, 1)
                    return
                split_mark[0] = mark(ins)

            ln_count = [0]

            def ln_stats(n, which):
                k = ln_count[0]
                ln_count[0] += 1
                if which == 0:
                    dve.wait_ge(x_in_sem[n], 16)
                for t in range(TB):
                    m = mark(nc.vector.bn_stats(stats[:, t, :], x[:, n * TB + t, :]))
                after(m)
                for t in range(TB):
                    m = mark(nc.vector.bn_aggr(mv[:, k % 2, t, :], stats[:, t, :]))
                after(m)
                nc.vector.tensor_scalar(var[:, k % 2, :], mv[:, k % 2, :, 1], EPS, None, ALU.add).then_inc(var_ready, 1)

            def ln_apply(n, which, k=None):
                k = ln_count[0] - 1 if k is None else k
                dve.wait_ge(rstd_ready, k + 1)
                to, ready = (xn1, xn1_ready) if which == 0 else (xn2, xn2_ready)
                if n > 0:
                    if which == 0:
                        dve.wait_ge(p0_full, p0("xn1t", n - 1) + 1)
                    else:
                        dve.wait_ge(rows_ready, n)
                for t in range(TB):
                    ins = nc.vector.tensor_scalar(to[:, t, :], x[:, n * TB + t, :], mv[:, k % 2, t, 0:1],
                                                  rstd[:, k % 2, t:t + 1], ALU.subtract, ALU.mult)
                ins.then_inc(ready, 1)

            def rope(n, i):
                qk, part = divmod(i, 2)
                dve.wait_ge(p1_full, p1("proj", (n, i)) + 1)
                if n > 0 and part == 0:
                    dve.wait_ge(split_ready, 2 * n)
                nc.vector.tensor_tensor((t1, t2)[part][:, qk, :], p1_bank[:, :], rot_sb[:, part, :],
                                        ALU.mult).then_inc(p1_read, 1)

            def rope0(i):
                qk, part = divmod(i, 2)
                dve.wait_ge(proj0_full, i + 1)
                nc.vector.tensor_tensor((t1, t2)[part][:, qk, :], proj0_bank[i][:, :], rot_sb[:, part, :],
                                        ALU.mult).then_inc(proj0_read, 1)

            def split0(qk, i):
                a, r = t1[:, qk, :], t2[:, qk, :]
                c = 3 * qk
                if i == 0:
                    dve.wait_ge(proj0_read, 2 * qk + 2)
                    ins = nc.vector.tensor_tensor(a, a, r, ALU.add)
                else:
                    after(split0_mark[qk])
                    if i == 1:
                        ins = nc.vector.tensor_copy(parts[:, c, :], a)
                    elif i == 2:
                        ins = nc.vector.tensor_tensor(r, a, parts[:, c, :], ALU.subtract)
                    elif i == 3:
                        ins = nc.vector.tensor_copy(parts[:, c + 1, :], r)
                    else:
                        nc.vector.tensor_tensor(parts[:, c + 2, :], r, parts[:, c + 1, :],
                                                ALU.subtract).then_inc(split_ready, 1)
                        return
                split0_mark[qk] = mark(ins)

            split0_mark = [0, 0]

            def normalise(u):
                b, g = divmod(u, UB)
                dve.wait_ge(p1_full, p1("ott", u) + 1)
                v = p1_bank[:, :].rearrange("p (t j c) -> p t j c", t=TB, c=VC)
                link(nc.vector.reciprocal(rc[:, :, :], v[:, :, :, D]))
                if g == 0 and b > 0:
                    dve.wait_ge(p0_full, p0("attnt", b - 1) + 1)
                nc.vector.tensor_tensor(
                    attn[:, :, g * HU * D:(g + 1) * HU * D].rearrange("p t (j d) -> p t j d", d=D),
                    v[:, :, :, 0:D], rc[:, :, :].unsqueeze(3).broadcast_to([P, TB, HU, D]),
                    ALU.mult).then_inc(norm_done, 1)
                dve.wait_ge(norm_done, u + 1)
                dve.sem_inc(p1_read, 1)

            def residual(b):
                dve.wait_ge(p1_full, p1("wo", b) + 1)
                xs = x[:, b * TB:(b + 1) * TB, :]
                nc.vector.tensor_tensor(xs, xs, p1_bank[:, :].rearrange("p (t e) -> p t e", e=E),
                                        ALU.add).then_inc(p1_read, 1)
                dve.wait_ge(p1_read, p1("wo", b) + 1)
                ln_stats(b, 1)

            def route(b):
                dve.wait_ge(p1_full, p1("logits", b) + 1)
                dve.wait_ge(c_loaded, 48)
                nc.vector.tensor_copy(lg[:, :, :], p1_bank[:, 0:TB * NE].rearrange("p (t e) -> p t e", e=NE)
                                      ).then_inc(p1_read, 1)
                dve.wait_ge(p1_read, p1("logits", b) + 1)
                if b > 0:
                    dve.wait_ge(tanh_ready, b)
                nc.vector.tensor_reduce(mx4[:, :], lg[:, :, :], AX.X, ALU.max).then_inc(mx4_ready, 1)
                dve.wait_ge(mx4_ready, b + 1)
                link(nc.vector.tensor_tensor(eq[:, :, :], lg[:, :, :],
                                             mx4[:, :].unsqueeze(2).broadcast_to([P, TB, NE]), ALU.is_equal))
                link(nc.vector.tensor_tensor(eq[:, :, :], eq[:, :, :],
                                             small[:, 0:NE].unsqueeze(1).broadcast_to([P, TB, NE]), ALU.mult))
                link(nc.vector.tensor_reduce(c4[:, :], eq[:, :, :], AX.X, ALU.max))
                nc.vector.tensor_tensor(onehot[:, b * TB:(b + 1) * TB, :], eq[:, :, :],
                                        c4[:, :].unsqueeze(2).broadcast_to([P, TB, NE]),
                                        ALU.is_equal).then_inc(onehot_ready, 1)

            def expert_rows(b):
                dve.wait_ge(tanh_ready, b + 1)
                link(nc.vector.tensor_scalar(sg4[:, :], th[:, :], 0.5, 0.5, ALU.mult, ALU.add))
                if b == 0:
                    dve.wait_ge(ids_done, 1)
                nc.vector.tensor_tensor(rows[:, b * TB:(b + 1) * TB, 0:E], xn2[:, :, :],
                                        sg4[:, :].unsqueeze(2).broadcast_to([P, TB, E]),
                                        ALU.mult).then_inc(rows_ready, 1)

            nc.vector.memset(half[:, :], -0.5).then_inc(half_done, 1)
            nc.vector.memset(vaug[:, :, :, :], 0.0).then_inc(vones_done, 1)
            ln_stats(0, 0)
            ln_stats(1, 0)
            ln_apply(0, 0, 0)
            dve.wait_ge(vones_done, 1)
            nc.vector.memset(vaug[:, :, :, D], 1.0).then_inc(vones_done, 1)
            ln_apply(1, 0, 1)
            dve.wait_ge(rot_loaded, 16)
            rope0(0)
            rope0(1)
            for i in range(3):
                split0(0, i)
            rope0(2)
            for i in range(3, 5):
                split0(0, i)
            rope0(3)
            for i in range(5):
                split0(1, i)
            for i in range(4):
                rope(1, i)
            for i in range(NC):
                reduce_chunk(0, i)
            for i in range(4):
                split_maxima(0, i)
            for i in range(NC):
                reduce_chunk(1, i)
            for u in range(STEPS):
                b, g = divmod(u, UB)
                todo = extras(u)
                for i in range(NC):
                    if u + 2 < U:
                        reduce_chunk(u + 2, i)
                    if u + 1 < U and i < 4:
                        split_maxima(u + 1, i)
                    for at, name, arg in todo:
                        if min(at + 1, NC - 1) != i:
                            continue
                        if name == "proj":
                            rope(*arg)
                        elif name == "ott":
                            normalise(arg)
                        elif name == "wo":
                            residual(arg)
                        elif name == "logits":
                            route(arg)
                    if g == 1 and b > 0 and i == 2:
                        ln_apply(b - 1, 1)
                    if g == 2 and b > 0 and i == 5:
                        expert_rows(b - 1)
                    if g == 1 and b + 2 < B and i == 8:
                        ln_stats(b + 2, 0)
                    if g == 2 and b + 2 < B and i == 1:
                        ln_apply(b + 2, 0)
            expert_rows(B - 1)

            def shared_mul(b):
                for c in range(2):
                    dve.wait_ge(sh_silu, 2 * b + c + 1)
                    dve.wait_ge(sh_full, 4 * b + 2 + c + 1)
                    if b > 1:
                        dve.wait_ge(shd_full, b - 1)
                    nc.vector.tensor_tensor(shh[:, b % 2, c, :], b_bank[c][:, :], shg[:, c, :],
                                            ALU.mult).then_inc(sh_mul, 1)

            def shared_add(b):
                dve.wait_ge(shd_full, b + 1)
                xs = x[:, b * TB:(b + 1) * TB, :]
                nc.vector.tensor_tensor(xs, xs, b_bank[2][:, :].rearrange("p (t e) -> p t e", e=E),
                                        ALU.add).then_inc(base_done, 1)

            shared_mul(0)
            dve.wait_ge(rank_full, 1)
            link(nc.vector.tensor_tensor(cmp16[:, :], p0_bank[0:NE, 0:NE], small[0:NE, NE:2 * NE], ALU.is_gt))
            link(nc.vector.tensor_reduce(tsum[:, :], cmp16[:, :], AX.X, ALU.add))
            nc.vector.tensor_scalar(tsb[:, :], rankc[0:NE, P:2 * P], tsum[:, 0:1], None,
                                    ALU.mult).then_inc(tsb_ready, 1)
            dve.wait_ge(base_full, 1)
            link(nc.vector.tensor_scalar(base[:, :], p0_bank[:, 0:2 * NE], float(P), None, ALU.mult))
            link(nc.vector.tensor_tensor(rk[:, :, :], p1_bank[:, 0:T * NE].rearrange("p (t e) -> p t e", e=NE),
                                         base[:, 0:NE].unsqueeze(1).broadcast_to([P, T, NE]), ALU.add))
            link(nc.vector.tensor_tensor(rk[:, :, :], rk[:, :, :], onehot[:, :, :], ALU.mult))
            link(nc.vector.tensor_reduce(posf[:, :], rk[:, :, :], AX.X, ALU.add))
            nc.vector.tensor_copy(posi[:, :], posf[:, :]).then_inc(pos_ready, 1)
            link(nc.vector.tensor_tensor(cmpt[:, :, :], base[0:1, NE:2 * NE].unsqueeze(1).broadcast_to([1, NT, NE]),
                                         small[0:1, 4 * NE:4 * NE + NT].unsqueeze(2).broadcast_to([1, NT, NE]),
                                         ALU.is_le))
            link(nc.vector.tensor_reduce(expf[:, :], cmpt[:, :, :], AX.X, ALU.add))
            nc.vector.tensor_scalar(expi[:, :], expf[:, :], float(NE - 1), None, ALU.min).then_inc(experts_ready, 1)
            for b in range(1, B):
                shared_mul(b)
                shared_add(b - 1)
            shared_add(B - 1)

            def tile_ids(r, k):
                dve.wait_ge(xin_loaded[k % RING], 16 * (r + k // RING + 1))
                nc.vector.tensor_copy(ids[:, bass.ds(r * RING + k, 1)],
                                      xin[:, k % RING, E:ROW].bitcast(I32)).then_inc(ids_ready, 1)

            def tile_mul(r, k, fill=False):
                dve.wait_ge(silu_ready, r * RING + (k + 1))
                if not fill:
                    dve.wait_ge(ht_full, r * RING + (k - 1))
                nc.vector.tensor_tensor(hh[:, k % 2, :], a_bank[k % 2][:, F:2 * F], sg[:, k % 2, :],
                                        ALU.mult).then_inc(hh_ready, 1)

            def tile_ht(r, k, fill=False):
                dve.wait_ge(ht_full, r * RING + (k + 1))
                if not fill:
                    dve.wait_ge(y_full, r * RING + (k - 1))
                nc.vector.tensor_copy(ht[:, k % 2, :, :],
                                      b_bank[k % 2][:, 0:F].rearrange("p (c n) -> p c n", c=2)).then_inc(ht_ready, 1)

            def slot(r, k, n=2 * RING, end=False):
                if n >= 2 and not (end and k > 1):
                    tile_mul(r, k - 2, n < 4)
                if n >= 3 and not (end and k > 2):
                    tile_ht(r, k - 3, n < 5)
                if not end:
                    tile_ids(r, k)

            for k in range(2 * RING):
                slot(0, k, k)
            with dve.Fori(2, NT // RING) as r:
                for k in range(RING):
                    slot(r, k)
            for k in range(3):
                slot(NT // RING, k, end=True)
            for b in range(B):
                dve.wait_ge(yl_loaded[b], 16)
                xs = x[:, b * TB:(b + 1) * TB, :]
                nc.vector.tensor_tensor(xs, xs, yl[:, b * TB:(b + 1) * TB, :], ALU.add).then_inc(final_ready, 1)

        @block.gpsimd
        def _(pool):
            step = [0]
            ln = [0]

            def root():
                k = ln[0]
                ln[0] += 1
                pool.wait_ge(half_done, 1)
                pool.wait_ge(var_ready, k + 1)
                nc.gpsimd.tensor_tensor(rstd[:, k % 2, :], var[:, k % 2, :], half[:, :], ALU.pow).then_inc(rstd_ready, 1)

            def split(n, qk, i):
                a, r = t1[:, qk, :], t2[:, qk, :]
                c = 3 * qk
                if i == 0:
                    pool.wait_ge(p1_read, p1("proj", (n, 2 * qk + 1)) + 1)
                else:
                    pool.wait_ge(split_step, step[0])
                if i == 0:
                    ins = nc.gpsimd.tensor_tensor(a, a, r, ALU.add)
                elif i == 1:
                    pool.wait_ge(parts_sent, 96 * n)
                    ins = nc.gpsimd.tensor_copy(parts[:, c, :], a)
                elif i == 2:
                    ins = nc.gpsimd.tensor_tensor(r, a, parts[:, c, :], ALU.subtract)
                elif i == 3:
                    ins = nc.gpsimd.tensor_copy(parts[:, c + 1, :], r)
                else:
                    nc.gpsimd.tensor_tensor(parts[:, c + 2, :], r, parts[:, c + 1, :],
                                            ALU.subtract).then_inc(split_ready, 1)
                    return
                ins.then_inc(split_step, 1)
                step[0] += 1

            def select(u, kt):
                w, off = S - kt * P, PT_OFF[kt]
                pool.wait_ge(b_read, NC * u + LAST_CHUNK[kt] + 1)
                v = pt[:, u % 2, off:off + HU * w].rearrange("p (j w) -> p j w", j=HU)[:, :, 0:P]
                nc.gpsimd.affine_select(out=v, in_=v, pattern=[[0, HU], [1, P]], compare_op=ALU.is_ge,
                                        fill=fill, base=0, channel_multiplier=-1).then_inc(masked, 1)

            fill = pool.to_reg(0.0)
            root()
            root()
            pool.wait_ge(rstd_ready, 2)
            nc.gpsimd.memset(kst[32:64, :, :].bitcast(I32), 0).then_inc(zeros_done, 1)
            pool.wait_ge(zeros_done, 1)
            nc.gpsimd.memset(qst[32:64, :, :].bitcast(I32), 0).then_inc(zeros_done, 1)
            pool.wait_ge(zeros_done, 2)
            nc.gpsimd.iota(rows[:, :, E:ROW].bitcast(I32), [[P, T]], base=0, channel_multiplier=1).then_inc(ids_done, 1)
            nc.gpsimd.memset(zrow[:, 0:E], 0.0).then_inc(zrow_done, 1)
            nc.gpsimd.memset(zrow[:, E:ROW].bitcast(I32), NOBODY).then_inc(zrow_done, 1)
            for qk in range(2):
                for i in range(5):
                    split(1, qk, i)
            for u in range(U):
                b, g = divmod(u, UB)
                if g == 1 and b > 0:
                    root()
                n, qk = (b + 2, 0) if g == 3 else (b + 1, 1)
                splits = g in (0, 3) and 2 <= n < B
                select(u, 0)
                if splits:
                    for i in range(3):
                        split(n, qk, i)
                select(u, 1)
                if splits:
                    for i in range(3, 5):
                        split(n, qk, i)
                select(u, 2)
                if g == 1 and b + 2 < B:
                    root()
                select(u, 3)
            root()
            bound = pool.to_reg(NT * P - 1)
            token_bound = pool.to_reg(B * S - 1)
            pool.wait_ge(table_cleared, 16)
            pool.wait_ge(rows_ready, B)
            pool.wait_ge(pos_ready, 1)
            for t in range(T):
                nc.gpsimd.indirect_dma_start(rows_scr.ap(), bass.IndirectOffsetOnAxis(ap=posi[:, t:t + 1], axis=0),
                                             rows[:, t, :], None, bounds_check=bound,
                                             oob_is_err=False).then_inc(scattered, 16)
            for i in range(NT):
                pool.wait_ge(ids_ready, i + 1)
                pool.wait_ge(y_ready, i + 1)
                nc.gpsimd.indirect_dma_start(y_scr.ap(), bass.IndirectOffsetOnAxis(ap=ids[:, i:i + 1], axis=0),
                                             yt[:, i % RING, :], None, bounds_check=token_bound,
                                             oob_is_err=False).then_inc(y_sent[i % RING], 16)


def constants():
    import numpy as np
    f4, bf = np.float32, mybir.dt.np(BF16)
    inv = (1.0 / (f4(10000.0) ** (np.arange(0, D, 2, dtype=f4) / f4(D)))).astype(f4)
    freqs = np.outer(np.arange(S, dtype=f4), inv).astype(f4)
    emb = np.concatenate([freqs, freqs], -1)
    sign = np.where(np.arange(D) % 2 == 0, -1.0, 1.0).astype(f4)
    cos = np.repeat(np.cos(emb).T.astype(f4), H, axis=0)
    sin = np.repeat((np.sin(emb) * sign).T.astype(f4), H, axis=0)
    i = np.arange(P)
    mask = np.where(i[None, :] > i[:, None], -1e30, 0.0)
    ident_mask = np.stack([np.eye(P)] + [mask] * HU, axis=1).astype(bf)
    sel = np.zeros((3, HU, UB, HU, S))
    for j in range(HU):
        sel[:, j, :, j, :] = 1.0
    sel = sel.reshape(3 * HU, H, S).astype(bf)
    rank = np.zeros((P, 3 * P))
    rank[:, 0:P] = i[:, None] < i[None, :]
    rank[:, P:2 * P] = 1.0
    e = np.arange(NE)
    rank[0:NE, 2 * P:2 * P + NE] = e[:, None] < e[None, :]
    rank[0:NE, 2 * P + NE:2 * P + 2 * NE] = e[:, None] <= e[None, :]
    small = np.zeros((P, 4 * NE + 2 * NT), f4)
    small[:, 0:NE] = NE - e
    small[:, NE:2 * NE] = P * e
    small[:, 4 * NE:4 * NE + NT] = P * np.arange(NT)
    return {
        "rot": np.stack([cos, sin], axis=1), "ident": np.eye(P, dtype=f4), "ident_mask": ident_mask,
        "sel": sel, "rank": rank.astype(bf), "small": small,
    }


def kernel(L0_attn_x, L0_attn_Wq, L0_attn_Wk, L0_attn_Wv, L0_attn_Wo, L0_ffn_w_router, L0_ffn_gate_up_proj,
           L0_ffn_down_proj, L0_ffn_w_gate, L0_ffn_w_up, L0_ffn_w_down):
    import numpy as np
    import concourse.bacc as bacc
    from concourse.bass_utils import run_bass_kernel_spmd

    d_h = np.arange(H * D).reshape(H, D).T.reshape(-1)
    swapped = (np.arange(H * D) ^ 1).reshape(H, D).T.reshape(-1)
    wq, wk = np.asarray(L0_attn_Wq), np.asarray(L0_attn_Wk)
    c = constants()
    arrays = {
        "x": np.asarray(L0_attn_x),
        "w_att": np.stack([wq[d_h].T, wq[swapped].T, wk[d_h].T, wk[swapped].T,
                           np.asarray(L0_attn_Wv).T, np.asarray(L0_attn_Wo).T], axis=1),
        "w_router": np.asarray(L0_ffn_w_router).T,
        "w_gu": np.asarray(L0_ffn_gate_up_proj), "w_dn": np.asarray(L0_ffn_down_proj),
        "w_sh": np.concatenate([np.asarray(L0_ffn_w_gate).T, np.asarray(L0_ffn_w_up).T], axis=1),
        "w_shd": np.asarray(L0_ffn_w_down).T,
        **c,
    }
    arrays = {"in_" + k: np.ascontiguousarray(v) for k, v in arrays.items()}
    nc = bacc.Bacc("TRN2", target_bir_lowering=False, num_devices=1)
    args = [nc.dram_tensor(k, v.shape, mybir.dt.from_np(v.dtype), kind="ExternalInput").ap()
            for k, v in arrays.items()]
    out = nc.dram_tensor("out", (B, S, E), F32, kind="ExternalOutput").ap()
    block_kernel(nc, *args, out)
    result = run_bass_kernel_spmd(nc, [arrays], core_ids=[0])
    return result.results[0]["out"]
```

```python
from contextlib import ExitStack

import concourse.bass as bass
from concourse import mybir

F32 = mybir.dt.float32
BF16 = mybir.dt.bfloat16
I32 = mybir.dt.int32
ALU = mybir.AluOpType
ACT = mybir.ActivationFunctionType
AX = mybir.AxisListType

P = 128
B, S, E = 4, 512, 128
H, D = 16, 8
NE, F = 16, 256
T = B * S // P
TB = S // P
HU = 4
UB = H // HU
U = B * UB
SCALE = float(D) ** -0.5
EPS = 1e-5
PARTS = 6
KS = PARTS * D
MROW = 64
KM = MROW + 3 * HU
VC = 32
NT = B * S // P + NE - 1
ROW = 2 * E + 1
NOBODY = 1 << 20
RING = 8
ROUNDS = NT // RING
YRING = 4
EARLY = 8

CHUNKS = [(3, h, 1) for h in range(4)] + [(2, h, 1) for h in range(4)] + [(1, 0, 2), (1, 2, 2), (0, 0, 4)]
NC = len(CHUNKS)
PT_OFF = [0, HU * 512, HU * (512 + 384), HU * (512 + 384 + 256)]
PT_LEN = HU * (512 + 384 + 256 + 128)
LAST_CHUNK = [3, 7, 9, 10]


def width(block):
    return P * (block + 1)


def extras(u):
    b, g = divmod(u, UB)
    out = []
    if 0 < u < U:
        out += [(1, "pv", (u - 1, 2)), (2, "pv", (u - 1, 3)), (5, "ott", u - 1)]
    if g == 0 and 0 < b < B:
        out += [(3, "v", b)]
    if u + 1 < U:
        out += [(5, "mt", u + 1)]
    if u < U:
        out += [(6, "pv", (u, 0)), (10, "pv", (u, 1))]
    if g == 2 and b + 2 < B:
        out += [(7, "xn1t", b + 2)]
    if g == 3 and b + 2 < B:
        out += [(at, "proj", (b + 2, i)) for i, at in enumerate((0, 2, 7, 9))]
    if g == 0 and b > 0:
        out += [(8, "attnt", b - 1), (10, "wo", b - 1)]
    if g == 1 and b > 0:
        out += [(8, "xn2t", b - 1), (10, "logits", b - 1)]
    if g == 2 and b > 0:
        out += [(3, "rank", b - 1)]
    if u >= U - 2:
        k0 = (u - (U - 2)) * (EARLY // 2)
        out += [(at, "early", k0 + k) for k, at in enumerate((0, 4, 7, 9))]
    return sorted(out, key=lambda x: x[0])


PROLOGUE = [("xn1t", 0), ("proj0", 0), ("xn1t", 1), ("v", 0), ("proj1", 1), ("mt", 0)]
LAST = B - 1
WARM_TILES = 7
WARM_MT = 8
WARM_STACKS = 6
WARM_START = 4
SCATTERS_BEFORE_ROOT = 0
TAIL = [("pv", (U - 1, 2)), ("pv", (U - 1, 3)), ("silu", (0, 0)), ("gate", (2, 0)), ("silu", (0, 1)),
        ("ott", U - 1), ("mul", (0, 0)), ("mul", (0, 1)), ("attnt", LAST), ("silu", (1, 0)), ("gate", (2, 1)),
        ("silu", (1, 1)), ("wo", LAST), ("down", 0), ("add", 0), ("mul", (1, 0)), ("mul", (1, 1)),
        ("norm2", LAST), ("up", (2, 0)), ("silu", (2, 0)), ("up", (2, 1)), ("silu", (2, 1)), ("mul", (2, 0)),
        ("down", 1), ("xn2t", LAST), ("add", 1), ("mul", (2, 1)), ("logits", LAST), ("gate", (3, 0)),
        ("gate", (3, 1)), ("rank", LAST), ("place", (0, 1, 2)), ("silu", (3, 0)), ("down", 2), ("up", (3, 0)),
        ("up", (3, 1)), ("place", (3,)), ("add", 2), ("place", (4,)), ("expert_rows", LAST), ("place", (5,)),
        ("silu", (3, 1)), ("mul", (3, 0)), ("place", (6,)), ("mul", (3, 1)), ("down", 3), ("place", (7, 8)),
        ("add", 3), ("place", (9, 10))]
ORDER = PROLOGUE + [(t, a) for u in range(U) for _, t, a in extras(u)] + TAIL
LAYERNORMS = [(0, 0), (1, 0), (2, 0), (0, 1), (3, 0), (1, 1), (2, 1), (3, 1)]
P0_USES = [x for x in ORDER if x[0] in ("xn1t", "v", "mt", "attnt", "xn2t")]
P1_USES = [x for x in ORDER if x[0] in ("proj", "ott", "wo", "logits", "rank")]


def p0(task, arg):
    return P0_USES.index((task, arg))


def p1(task, arg):
    return P1_USES.index((task, arg))


def block_kernel(nc, x_in, w_att_in, w_router, w_gu, w_dn, w_sh, w_shd, rot_in, ident_in, ident_mask_in,
                 sel_in, rank_in, small_in, out):
    q_scr = nc.dram_tensor("q_scr", [2, KS, H, S], BF16)
    k_scr = nc.dram_tensor("k_scr", [2, KS, H, S], BF16)
    rows_scr = nc.dram_tensor("rows_scr", [NT * P, ROW], F32)
    x_dram = x_in.rearrange("b (t p) d -> b p t d", p=P)
    out_rows = out.rearrange("b s d -> (b s) d")

    with ExitStack() as ctx:
        def sb(name, shape, dt=F32):
            return ctx.enter_context(nc.sbuf_tensor(name, shape, dt))

        def sem(name):
            return ctx.enter_context(nc.semaphore(name))

        def bank(name):
            return ctx.enter_context(nc.psum_tensor(name, [P, 512], F32))

        qst = sb("qst", [P, H, S], BF16)
        kst = sb("kst", [P, H, S], BF16)
        pt = sb("pt", [P, 2, PT_LEN])
        wgu_sb = sb("wgu_sb", [P, NE, 2 * F])
        wdn_sb = sb("wdn_sb", [P, NE, 2, E])
        vaug = sb("vaug", [P, TB, H, VC])
        xn2t = sb("xn2t", [P, B * S])
        rows = sb("rows", [P, T, ROW])
        x = rows[:, :, E:2 * E]
        xnt = sb("xnt", [P, 2, S])
        xn1 = sb("xn1", [P, TB, E])
        xn2 = sb("xn2", [P, TB, E])
        rot_sb = sb("rot_sb", [P, 2, S])
        t1 = sb("t1", [P, 2, S])
        t2 = sb("t2", [P, 2, S])
        parts = sb("parts", [P, 6, S], BF16)
        ots = sb("ots", [P, S])
        attn = sb("attn", [P, TB, H * D])
        attnt = sb("attnt", [P, S])
        w_att = sb("w_att", [P, 6, E])
        wr_sb = sb("wr_sb", [P, NE])
        wsh_sb = sb("wsh_sb", [P, 2 * F])
        wshd_sb = sb("wshd_sb", [P, 2, E])
        ident = sb("ident", [P, P])
        ident_mask = sb("ident_mask", [P, 1 + HU, P], BF16)
        identb, mask = ident_mask[:, 0, :], ident_mask[:, 1:1 + HU, :]
        rankc = sb("rankc", [P, 3 * P], BF16)
        small = sb("small", [P, 2 * NE + NE * NE + NT])
        ties = small[:, 0:NE]
        full = small[:, NE:2 * NE]
        upto = small[:, 2 * NE:2 * NE + NE * NE].rearrange("p (e f) -> p e f", f=NE)
        tile_row = small[0:1, 2 * NE + NE * NE:]
        mx = sb("mx", [P, 2, TB, HU])
        mres = sb("mres", [P, TB, HU])
        mparts = sb("mparts", [P, TB, 3, HU], BF16)
        m12 = sb("m12", [3 * HU, S], BF16)
        stats = sb("stats", [P, TB, 6])
        mv = sb("mv", [P, 2, TB, 2])
        var = sb("var", [P, 2, TB])
        rstd = sb("rstd", [P, 2, TB])
        half = sb("half", [P, TB])
        rc = sb("rc", [P, TB, HU])
        lg = sb("lg", [P, TB, NE])
        eq = sb("eq", [P, TB, NE])
        mx4 = sb("mx4", [P, TB])
        c4 = sb("c4", [P, TB])
        th = sb("th", [P, TB])
        sg4 = sb("sg4", [P, TB])
        onehot = sb("onehot", [P, T, NE], BF16)
        zrow = sb("zrow", [P, ROW])
        pair = sb("pair", [P, NE, NE])
        count = sb("count", [P, NE])
        tiles = sb("tiles", [P, NE])
        tiles_new = sb("tiles_new", [P, NE])
        added = sb("added", [P, NE])
        ends = sb("ends", [P, NE])
        end_row = sb("end_row", [P, 1])
        shift = sb("shift", [P, NE])
        shift_new = sb("shift_new", [P, NE])
        dshift = sb("dshift", [P, NE])
        room = sb("room", [P, NE])
        start = sb("start", [P, NE])
        grown = sb("grown", [P, NE])
        rk = sb("rk", [P, TB, NE])
        past = sb("past", [P, TB, NE])
        posf = sb("posf", [P, TB])
        posi = sb("posi", [P, T], I32)
        cmpt = sb("cmpt", [1, NT, NE])
        exps = sb("exps", [1, NT])
        expf = sb("expf", [1, NT])
        expi = sb("expi", [1, NT], I32)
        shg = pt[:, 0, 0:1024].rearrange("p (c n) -> p c n", c=2)
        shh = pt[:, 0, 1024:3072].rearrange("p (r c n) -> p r c n", r=2, c=2)
        xt = pt[:, 0, 3072:3328].rearrange("p (r n) -> p r n", r=2)
        sg = pt[:, 0, 3328:3840].rearrange("p (r n) -> p r n", r=2)
        hh = pt[:, 0, 3840:4352].rearrange("p (r n) -> p r n", r=2)
        ht = pt[:, 0, 4352:4864].rearrange("p (r c n) -> p r c n", r=2, c=2)
        xin = pt[:, 1, 0:RING * ROW].rearrange("p (r n) -> p r n", r=RING)
        yt = pt[:, 1, RING * ROW:RING * ROW + YRING * E].rearrange("p (r n) -> p r n", r=YRING)

        a_bank = [bank("a0"), bank("a1")]
        b_bank = [bank("b0"), bank("b1"), bank("b2")]
        ot_bank = bank("ot")
        p0_bank = bank("p0")
        p1_bank = bank("p1")
        a_ring, b_ring = a_bank + b_bank[2:3], b_bank[0:2]
        proj0_bank = a_bank + b_bank[0:2]
        proj1_bank = [p1_bank, b_bank[2], ot_bank, a_bank[0]]
        early_sb = ([t1[:, c, :] for c in range(2)] + [t2[:, c, :] for c in range(2)]
                    + [xnt[:, c, :] for c in range(2)]
                    + [parts[:, 2 * c:2 * c + 2, :].rearrange("p c s -> p (c s)").bitcast(F32) for c in range(2)])
        last_banks = [b_bank[2], ot_bank] + a_bank
        mt_view = p0_bank[0:3 * HU, 0:S // 2].bitcast(BF16)

        x_in_sem = [sem(f"x_loaded{b}") for b in range(B)]
        ident_loaded = sem("ident_loaded")
        w_loaded = sem("w_loaded")
        rot_loaded = sem("rot_loaded")
        mask_loaded = sem("mask_loaded")
        proj0_full = sem("proj0_full")
        proj0_read = sem("proj0_read")
        proj1_full = sem("proj1_full")
        proj1_read = sem("proj1_read")
        rest_ready = sem("rest_ready")
        part_cast = sem("part_cast")
        c_loaded = sem("c_loaded")
        wexp_loaded = sem("wexp_loaded")
        sel_loaded = sem("sel_loaded")
        zeros_done = sem("zeros_done")
        vones_done = sem("vones_done")
        ots_cleared = sem("ots_cleared")
        books_cleared = sem("books_cleared")
        half_done = sem("half_done")
        zrow_done = sem("zrow_done")
        table_cleared = sem("table_cleared")
        ids_done = sem("ids_done")
        var_ready = sem("var_ready")
        rstd_ready = sem("rstd_ready")
        centred = sem("centred")
        xn1_ready = sem("xn1_ready")
        xn2_ready = sem("xn2_ready")
        p0_full = sem("p0_full")
        p0_read = sem("p0_read")
        p1_full = sem("p1_full")
        p1_read = sem("p1_read")
        split_ready = sem("split_ready")
        split_step = sem("split_step")
        parts_sent = sem("parts_sent")
        slot_loaded = [sem(f"slot_loaded{g}") for g in range(UB)]
        a_full = sem("a_full")
        a_read = sem("a_read")
        b_full = sem("b_full")
        b_read = sem("b_read")
        masked = sem("masked")
        pv_done = sem("pv_done")
        ot_read = sem("ot_read")
        mparts_ready = sem("mparts_ready")
        mrow_loaded = [sem("mrow_loaded0"), sem("mrow_loaded1")]
        norm_done = sem("norm_done")
        tanh_ready = sem("tanh_ready")
        mx4_ready = sem("mx4_ready")
        rows_ready = sem("rows_ready")
        onehot_ready = sem("onehot_ready")
        experts_ready = sem("experts_ready")
        pos_ready = sem("pos_ready")
        scattered = sem("scattered")
        sh_silu = sem("sh_silu")
        sh_mul = sem("sh_mul")
        wsh_loaded = sem("wsh_loaded")
        early_full = sem("early_full")
        early_read = sem("early_read")
        sg4_ready = sem("sg4_ready")
        last_rows_ready = sem("last_rows_ready")
        gate_full = sem("gate_full")
        up_full = sem("up_full")
        down_full = sem("down_full")
        base_done = sem("base_done")
        xin_loaded = [sem(f"xin_loaded{i}") for i in range(RING)]
        xt_full = sem("xt_full")
        xt_ready = sem("xt_ready")
        h_full = sem("h_full")
        silu_ready = sem("silu_ready")
        hh_ready = sem("hh_ready")
        ht_full = sem("ht_full")
        ht_ready = sem("ht_ready")
        y_full = sem("y_full")
        y_ready = sem("y_ready")
        y_sent = [sem(f"y_sent{i}") for i in range(YRING)]
        v_chain = sem("v_chain")
        v_copied = sem("v_copied")

        block = ctx.enter_context(nc.Block())

        @block.sync
        def _(sp):
            for b in range(B):
                sp.dma_start(x[:, b * TB:(b + 1) * TB, :], x_dram[b]).then_inc(x_in_sem[b], 16)
                if b == 0:
                    sp.dma_start(ident[:], ident_in).then_inc(ident_loaded, 16)
                if b == 1:
                    sp.dma_start(w_att[:], w_att_in).then_inc(w_loaded, 16)
                    sp.dma_start(rot_sb[:], rot_in).then_inc(rot_loaded, 16)
                    sp.dma_start(ident_mask[:], ident_mask_in).then_inc(mask_loaded, 16)
            sp.wait_ge(zeros_done, 2)
            sp.dma_start(kst[MROW:KM, :, :], sel_in).then_inc(sel_loaded, 16)

            def send_parts(n):
                par = n % 2
                sp.wait_ge(split_ready, 2 * n + 1)
                q_to = q_scr.ap()[par].rearrange("(r d) h t -> (d h) r t", d=D)
                k_to = k_scr.ap()[par].rearrange("(r d) h t -> (d h) r t", d=D)
                for to, r0, c, rep in ((q_to, 0, 0, 3), (q_to, 3, 1, 2), (q_to, 5, 2, 1)):
                    sp.dma_start(to[:, r0:r0 + rep, :],
                                 parts[:, c:c + 1, :].broadcast_to([P, rep, S])).then_inc(parts_sent, 16)
                sp.wait_ge(split_ready, 2 * n + 2)
                for to, r0, c, n_c in ((k_to, 0, 3, 3), (k_to, 3, 3, 2), (k_to, 5, 3, 1)):
                    sp.dma_start(to[:, r0:r0 + n_c, :], parts[:, c:c + n_c, :]).then_inc(parts_sent, 16)
                sp.wait_ge(parts_sent, 96 * (n + 1))

            def load_slot(n, g):
                if n > 0:
                    sp.wait_ge(b_full, NC * (UB * (n - 1) + g + 1))
                hs = slice(HU * g, HU * g + HU)
                sp.dma_start(qst[0:KS, hs, :], q_scr.ap()[n % 2, :, hs, :]).then_inc(slot_loaded[g], 16)
                sp.dma_start(kst[0:KS, hs, :], k_scr.ap()[n % 2, :, hs, :]).then_inc(slot_loaded[g], 16)

            def load_maxima(u):
                g = u % UB
                sp.wait_ge(p0_read, p0("mt", u) + 1)
                if u >= UB:
                    sp.wait_ge(b_full, NC * (u - UB + 1))
                sp.dma_start(qst[MROW:KM, HU * g:HU * g + HU, :],
                             m12[:, :].rearrange("p (o s) -> p o s", o=1).broadcast_to([3 * HU, HU, S])
                             ).then_inc(mrow_loaded[u % 2], 16)

            send_parts(0)
            for g in range(UB):
                load_slot(0, g)
            sp.dma_start(wr_sb[:], w_router).then_inc(c_loaded, 16)
            sp.dma_start(rankc[:], rank_in).then_inc(c_loaded, 16)
            sp.dma_start(small[:], small_in).then_inc(c_loaded, 16)
            load_maxima(0)
            sp.dma_start(wsh_sb[:], w_sh).then_inc(wsh_loaded, 16)
            sp.dma_start(wshd_sb[:], w_shd.rearrange("(c p) h -> p c h", p=P)).then_inc(wsh_loaded, 16)
            sp.wait_ge(zrow_done, 2)
            for u in range(U):
                b, g = divmod(u, UB)
                if g > 0 and b + 1 < B:
                    load_slot(b + 1, g - 1)
                if g == 0 and b > 0:
                    load_slot(b, UB - 1)
                if u + 1 < U:
                    load_maxima(u + 1)
                if g == 0 and b + 1 < B:
                    send_parts(b + 1)
                if u < UB * 2:
                    part = -(-NT // (UB * 2))
                    n = min(part, NT - u * part)
                    sp.dma_start(rows_scr.ap().rearrange("(t p) c -> p t c", p=P)[:, u * part:u * part + n, :],
                                 zrow[:, :].rearrange("p (o c) -> p o c", o=1).broadcast_to([P, n, ROW])
                                 ).then_inc(table_cleared, 16)
                sp.dma_start(wgu_sb[:, u, :], w_gu[u]).then_inc(wexp_loaded, 16)
                sp.dma_start(wdn_sb[:, u, :, :], w_dn[u].rearrange("(c p) h -> p c h", p=P)).then_inc(wexp_loaded, 16)

            sp.wait_ge(scattered, 16 * T)

            def load_rows(r, k, first):
                if not first:
                    sp.wait_ge(y_sent[k % YRING], 16 * (r * (RING // YRING) + (k - RING) // YRING + 1))
                sp.dma_start(xin[:, k, :], rows_scr.ap()[bass.ds(r * (RING * P) + k * P, P), :]
                             ).then_inc(xin_loaded[k], 16)

            for k in range(RING):
                load_rows(0, k, True)
            with sp.Fori(1, ROUNDS) as r:
                for k in range(RING):
                    load_rows(r, k, False)
            for k in range(NT % RING):
                load_rows(ROUNDS, k, False)
            for k in range(YRING):
                sp.wait_ge(y_sent[k], 16 * ((NT - k + YRING - 1) // YRING))

        @block.tensor
        def _(pe):
            def a_chunk(u, i):
                block_, h0, n = CHUNKS[i]
                w, g, c = width(block_), u % UB, NC * u + i
                if i == 0:
                    pe.wait_ge(slot_loaded[g], 32 * (u // UB + 1))
                if c >= len(a_ring):
                    pe.wait_ge(a_read, c - len(a_ring) + 1)
                to = a_ring[c % len(a_ring)]
                for j in range(n):
                    h = HU * g + h0 + j
                    pe.matmul(to[:, j * w:(j + 1) * w], qst[0:MROW, h, block_ * P:(block_ + 1) * P],
                              kst[0:MROW, h, 0:w], start=(j == 0), stop=False, skip_group_check=True)
                diag = to[:, 0:n * w].rearrange("p (j w) -> p j w", j=n)[:, :, w - P:w]
                pe.matmul(diag, identb, mask[:, 0:n, :], start=False, stop=True,
                          skip_group_check=True).then_inc(a_full, 1)

            def b_chunk(u, i):
                block_, h0, n = CHUNKS[i]
                w, g, c, kt = width(block_), u % UB, NC * u + i, 3 - block_
                if i == 0:
                    pe.wait_ge(mrow_loaded[u % 2], 16 * (u // 2 + 1))
                    if u < 1:
                        pe.wait_ge(sel_loaded, 16)
                if c >= len(b_ring):
                    pe.wait_ge(b_read, c - len(b_ring) + 1)
                to = b_ring[c % len(b_ring)]
                for j in range(n):
                    h = HU * g + h0 + j
                    mm = pe.matmul(to[:, j * w:(j + 1) * w], kst[0:KM, h, kt * P:(kt + 1) * P],
                                   qst[0:KM, h, kt * P:S], start=True, stop=True)
                mm.then_inc(b_full, 1)

            def transposes(to, src):
                for t in range(TB):
                    mm = pe.transpose(to[:, t * P:(t + 1) * P], src[:, t, :], ident[:, :])
                return mm

            def task(name, arg):
                if (name, arg) in P0_USES:
                    if p0(name, arg) > 0:
                        pe.wait_ge(p0_read, p0(name, arg))
                if (name, arg) in P1_USES:
                    if p1(name, arg) > 0:
                        pe.wait_ge(p1_read, p1(name, arg))
                if name == "xn1t":
                    pe.wait_ge(xn1_ready, arg + 1)
                    transposes(p0_bank, xn1).then_inc(p0_full, 1)
                elif name in ("proj0", "proj1"):
                    pe.wait_ge(p0_read, p0("xn1t", arg) + 1)
                    if arg == 0:
                        pe.wait_ge(w_loaded, 16)
                    else:
                        pe.wait_ge(proj0_read, 1)
                    for i in range(4):
                        pe.matmul((proj0_bank, proj1_bank)[arg][i][:, :], w_att[:, i, :], xnt[:, arg, :], start=True,
                                  stop=True).then_inc((proj0_full, proj1_full)[arg], 1)
                elif name == "proj":
                    n, i = arg
                    pe.wait_ge(p0_read, p0("xn1t", n) + 1)
                    pe.matmul(p1_bank[:, :], w_att[:, i, :], xnt[:, n % 2, :], start=True,
                              stop=True).then_inc(p1_full, 1)
                elif name == "v":
                    for t in range(TB):
                        mm = pe.matmul(p0_bank[:, t * P:(t + 1) * P], xnt[:, arg % 2, t * P:(t + 1) * P],
                                       w_att[:, 4, :], start=True, stop=True)
                    mm.then_inc(p0_full, 1)
                elif name == "mt":
                    pe.wait_ge(mparts_ready, arg + 1)
                    for t in range(TB):
                        mm = pe.transpose(mt_view[:, t * P:(t + 1) * P],
                                          mparts[:, t, :, :].rearrange("p c h -> p (c h)"), identb)
                    mm.then_inc(p0_full, 1)
                elif name == "pv":
                    u, kt = arg
                    g, w, off = u % UB, S - kt * P, PT_OFF[kt]
                    pe.wait_ge(masked, TB * u + kt + 1)
                    if kt == 0:
                        pe.wait_ge(v_copied, u // UB + 1)
                        if u > 0:
                            pe.wait_ge(ot_read, u)
                    for j in range(HU):
                        mm = pe.matmul(ot_bank[32 * j:32 * j + VC, kt * P:S], vaug[:, kt, HU * g + j, :],
                                       pt[:, u % 2, off + j * w:off + (j + 1) * w],
                                       start=(kt == 0), stop=(kt == TB - 1), tile_position=(0, 32 * j))
                    mm.then_inc(pv_done, 1)
                elif name == "ott":
                    pe.wait_ge(ot_read, arg + 1)
                    transposes(p1_bank, ots[:, :].rearrange("p (t q) -> p t q", t=TB)).then_inc(p1_full, 1)
                elif name == "attnt":
                    pe.wait_ge(norm_done, UB * (arg + 1))
                    transposes(p0_bank, attn).then_inc(p0_full, 1)
                elif name == "wo":
                    pe.wait_ge(p0_read, p0("attnt", arg) + 1)
                    for t in range(TB):
                        mm = pe.matmul(p1_bank[:, t * P:(t + 1) * P], attnt[:, t * P:(t + 1) * P],
                                       w_att[:, 5, :], start=True, stop=True)
                    mm.then_inc(p1_full, 1)
                elif name == "xn2t":
                    pe.wait_ge(xn2_ready, arg + 1)
                    transposes(p0_bank, xn2).then_inc(p0_full, 1)
                elif name == "early":
                    b, kind, c = arg // 4, arg // 2 % 2, arg % 2
                    if arg == 0:
                        pe.wait_ge(wsh_loaded, 32)
                        pe.wait_ge(a_read, NC * U)
                    if arg >= len(a_ring):
                        pe.wait_ge(early_read, arg - len(a_ring) + 1)
                    pe.matmul(a_ring[arg % len(a_ring)][:, :], wsh_sb[:, kind * F + c * P:kind * F + (c + 1) * P],
                              xn2t[:, b * S:(b + 1) * S], start=True, stop=True).then_inc(early_full, 1)
                elif name == "gate":
                    b, c = arg
                    if b == EARLY // 4:
                        pe.wait_ge(early_read, EARLY)
                    else:
                        pe.wait_ge(sh_silu, 2 * (b - 1) + c + 1)
                    pe.matmul(a_bank[c][:, :], wsh_sb[:, c * P:(c + 1) * P], xn2t[:, b * S:(b + 1) * S],
                              start=True, stop=True).then_inc(gate_full, 1)
                elif name == "up":
                    b, c = arg
                    if b == EARLY // 4:
                        pe.wait_ge(b_read, NC * U)
                    else:
                        pe.wait_ge(sh_mul, 2 * (b - 1) + c + 1)
                    pe.matmul(b_bank[c][:, :], wsh_sb[:, F + c * P:F + (c + 1) * P],
                              xn2t[:, b * S:(b + 1) * S], start=True, stop=True).then_inc(up_full, 1)
                elif name == "down":
                    b = arg
                    pe.wait_ge(sh_mul, 2 * b + 2)
                    pe.wait_ge(early_read, EARLY)
                    if b > 0:
                        pe.wait_ge(base_done, b)
                    for t in range(TB):
                        to = (last_banks[t] if b == LAST else b_bank[2])[:, t * P:(t + 1) * P]
                        for c in range(2):
                            mm = pe.matmul(to, shh[:, b % 2, c, t * P:(t + 1) * P],
                                           wshd_sb[:, c, :], start=(c == 0), stop=(c == 1))
                        if b == LAST or t == TB - 1:
                            mm.then_inc(down_full, 1)
                elif name == "rank":
                    pe.wait_ge(onehot_ready, arg + 1)
                    r = p1_bank[:, 0:(TB + 1) * NE].rearrange("p (t e) -> p t e", e=NE)
                    hot = onehot[:, arg * TB:(arg + 1) * TB, :]
                    tri, ones = rankc[:, 0:P], rankc[:, P:2 * P]
                    pe.matmul(r, rankc[:, 2 * P:3 * P], hot[:, 0:1, :].broadcast_to([P, TB + 1, NE]),
                              start=True, stop=False, skip_group_check=True)
                    pe.matmul(r[:, 0:TB, :], tri, hot, start=False, stop=False, skip_group_check=True)
                    for t in range(TB):
                        mm = pe.matmul(r[:, t + 1:TB + 1, :], ones, hot[:, t:t + 1, :].broadcast_to([P, TB - t, NE]),
                                       start=False, stop=(t == TB - 1), skip_group_check=True)
                    mm.then_inc(p1_full, 1)
                elif name == "logits":
                    pe.wait_ge(p0_read, p0("xn2t", arg) + 1)
                    pe.wait_ge(c_loaded, 48)
                    for t in range(TB):
                        c = arg * TB + t
                        mm = pe.matmul(p1_bank[:, t * NE:(t + 1) * NE], xn2t[:, c * P:(c + 1) * P],
                                       wr_sb[:, :], start=True, stop=True)
                    mm.then_inc(p1_full, 1)

            pe.wait_ge(ots_cleared, 1)
            for _ in range(WARM_START):
                pe.matmul(p1_bank[:, :], ots[:, 0:P], ots[:, :], start=True, stop=True)
            pe.wait_ge(ident_loaded, 16)
            for name, arg in PROLOGUE:
                if name == "mt":
                    pe.wait_ge(proj0_read, 4)
                    pe.wait_ge(proj1_read, 4)
                    pe.wait_ge(p0_read, p0("v", 0) + 1)
                    for _ in range(WARM_STACKS):
                        pe.matmul(p0_bank[:, :], ots[:, 0:P], ots[:, :], start=True, stop=True)
                    pe.wait_ge(mask_loaded, 16)
                    for i in range(NC):
                        a_chunk(0, i)
                    for _ in range(WARM_MT):
                        pe.matmul(ot_bank[:, :], identb, mask[:, :, :], start=True, stop=True)
                    task(name, arg)
                    for i in range(NC):
                        a_chunk(1, i)
                else:
                    task(name, arg)
            for u in range(U):
                todo = extras(u)
                for i in range(NC):
                    b_chunk(u, i)
                    if u + 2 < U:
                        a_chunk(u + 2, i)
                    for after, name, arg in todo:
                        if after == i:
                            task(name, arg)

            for name, arg in TAIL:
                task(name, arg)
            pe.wait_ge(p0_read, len(P0_USES))
            for _ in range(WARM_TILES):
                pe.matmul(p0_bank[:, :], wsh_sb[:, 0:P], xn2t[:, 0:S], start=True, stop=True)

            x_bank, h_bank, ht_bank, y_bank = [p0_bank, p1_bank], a_bank, b_bank[0:2], [b_bank[2], ot_bank]

            expert_reg = [pe.alloc_register(f"expert{i}") for i in range(4)]

            def load_expert(r, k):
                pe.reg_load(expert_reg[k % 4], expi[0:1, bass.ds(r * RING + k, 1)])

            def expert_of(k):
                return pe.snap(expert_reg[k % 4], min_val=0, max_val=NE - 1)

            def tile_transpose(r, k, fill=False):
                pe.wait_ge(xin_loaded[k % RING], 16 * (r + k // RING + 1))
                if not fill:
                    pe.wait_ge(xt_ready, r * RING + (k - 1))
                pe.transpose(x_bank[k % 2][:, 0:P], xin[:, k % RING, 0:E], ident[:, :]).then_inc(xt_full, 1)

            def tile_up(r, k, e, fill=False):
                pe.wait_ge(xt_ready, r * RING + (k + 1))
                if not fill:
                    pe.wait_ge(hh_ready, r * RING + (k - 1))
                pe.matmul(h_bank[k % 2][:, :], xt[:, k % 2, :],
                          wgu_sb[:, bass.ds(e, 1), :].rearrange("p o f -> p (o f)"),
                          start=True, stop=True).then_inc(h_full, 1)

            def tile_hidden(r, k, fill=False):
                pe.wait_ge(hh_ready, r * RING + (k + 1))
                if not fill:
                    pe.wait_ge(ht_ready, r * RING + (k - 1))
                for c in range(2):
                    mm = pe.transpose(ht_bank[k % 2][:, c * P:(c + 1) * P], hh[:, k % 2, c * P:(c + 1) * P],
                                      ident[:, :])
                mm.then_inc(ht_full, 1)

            def tile_down(r, k, e, fill=False):
                pe.wait_ge(ht_ready, r * RING + (k + 1))
                if not fill:
                    pe.wait_ge(y_ready, r * RING + (k - 1))
                for c in range(2):
                    mm = pe.matmul(y_bank[k % 2][:, 0:E], ht[:, k % 2, c, :],
                                   wdn_sb[:, bass.ds(e, 1), c, :].rearrange("p o f -> p (o f)"),
                                   start=(c == 0), stop=(c == 1))
                mm.then_inc(y_full, 1)

            pe.wait_ge(experts_ready, 1)
            pe.wait_ge(wexp_loaded, 32 * NE)
            pe.wait_ge(base_done, LAST + TB)
            pe.wait_ge(p0_read, len(P0_USES))
            pe.wait_ge(p1_read, len(P1_USES))

            def slot(r, k, n=RING, end=False):
                if n >= 3 and not (end and k > NT % RING + 2):
                    tile_hidden(r, k - 3, n < 5)
                if n >= 4:
                    tile_down(r, k - 4, expert_of(k - 4), n < 6)
                if not end:
                    tile_transpose(r, k, n < 2)
                if n >= 1 and not (end and k > NT % RING):
                    tile_up(r, k - 1, expert_of(k - 1), n < 3)
                if not end:
                    load_expert(r, k)

            for k in range(RING):
                slot(0, k, k)
            with pe.Fori(1, ROUNDS) as r:
                for k in range(RING):
                    slot(r, k)
            for k in range(NT % RING):
                slot(ROUNDS, k)
            for k in range(NT % RING, NT % RING + 4):
                slot(ROUNDS, k, end=True)

        @block.scalar
        def _(act):
            def exp_chunk(u, i):
                block_, h0, n = CHUNKS[i]
                w, c, kt = width(block_), NC * u + i, 3 - block_
                act.wait_ge(b_full, c + 1)
                if i == 0 and u >= 2:
                    act.wait_ge(pv_done, TB * (u - 1))
                off = PT_OFF[kt] + h0 * w
                nc.scalar.activation(pt[:, u % 2, off:off + n * w], b_ring[c % len(b_ring)][:, 0:n * w], ACT.Exp,
                                     scale=SCALE).then_inc(b_read, 1)

            def task(name, arg):
                if name == "pv":
                    u, kt = arg
                    if kt == TB - 1:
                        act.wait_ge(pv_done, TB * (u + 1))
                        if u > 0:
                            act.wait_ge(p1_full, p1("ott", u - 1) + 1)
                        nc.scalar.copy(ots[:, :], ot_bank[:, :]).then_inc(ot_read, 1)
                    return
                if (name, arg) not in P0_USES:
                    return
                act.wait_ge(p0_full, p0(name, arg) + 1)
                if name == "xn1t":
                    nc.scalar.copy(xnt[:, arg % 2, :], p0_bank[:, :]).then_inc(p0_read, 1)
                elif name == "v":
                    if arg > 0:
                        act.wait_ge(pv_done, TB * UB * arg)
                    act.wait_ge(vones_done, 2)
                    nc.scalar.copy(vaug[:, :, :, 0:D],
                                   p0_bank[:, :].rearrange("p (t h d) -> p t h d", t=TB, d=D)).then_inc(v_copied, 1)
                    act.wait_ge(v_copied, arg + 1)
                    act.sem_inc(p0_read, 1)
                elif name == "mt":
                    if arg > 0:
                        act.wait_ge(mrow_loaded[(arg - 1) % 2], 16 * ((arg - 1) // 2 + 1))
                    nc.scalar.copy(m12[:, :], mt_view).then_inc(p0_read, 1)
                elif name == "attnt":
                    nc.scalar.copy(attnt[:, :], p0_bank[:, :]).then_inc(p0_read, 1)
                elif name == "xn2t":
                    nc.scalar.copy(xn2t[:, arg * S:(arg + 1) * S], p0_bank[:, :]).then_inc(p0_read, 1)

            def half_tanh(b):
                act.wait_ge(mx4_ready, b + 1)
                if b > 0:
                    act.wait_ge(sg4_ready, b)
                nc.scalar.activation(th[:, :], mx4[:, :], ACT.Tanh, scale=0.5).then_inc(tanh_ready, 1)

            def cast(k):
                qk, part = k % 2, k // 2
                act.wait_ge(rest_ready, k + 1)
                nc.scalar.copy(parts[:, 3 * qk + part, :], (t1, t2)[part][:, qk, :]).then_inc(part_cast, 1)

            for name, arg in PROLOGUE:
                if (name, arg) == ("v", 0):
                    for k in range(1, 4):
                        cast(k)
                task(name, arg)
                if (name, arg) == ("xn1t", 0):
                    cast(0)
            for u in range(U):
                b, g = divmod(u, UB)
                todo = extras(u)
                for i in range(NC):
                    exp_chunk(u, i)
                    for after, name, arg in todo:
                        if min(after + 1, NC - 1) == i:
                            task(name, arg)
                    if g == 2 and b > 0 and i == 2:
                        half_tanh(b - 1)
            for name, arg in TAIL:
                if name == "silu":
                    b, c = arg
                    if b < EARLY // 4:
                        gates = early_sb[4 * b + c]
                        act.wait_ge(early_read, EARLY)
                    else:
                        gates = a_bank[c][:, :]
                        act.wait_ge(gate_full, 2 * (b - EARLY // 4) + c + 1)
                    if b > 0:
                        act.wait_ge(sh_mul, 2 * (b - 1) + c + 1)
                    nc.scalar.activation(shg[:, c, :], gates, ACT.Silu).then_inc(sh_silu, 1)
                else:
                    task(name, arg)
                    if name == "xn2t":
                        half_tanh(arg)

            def tile_xt(r, k, fill=False):
                act.wait_ge(xt_full, r * RING + (k + 1))
                if not fill:
                    act.wait_ge(h_full, r * RING + (k - 1))
                nc.scalar.copy(xt[:, k % 2, :], [p0_bank, p1_bank][k % 2][:, 0:P]).then_inc(xt_ready, 1)

            def tile_silu(r, k, fill=False):
                act.wait_ge(h_full, r * RING + (k + 1))
                if not fill:
                    act.wait_ge(hh_ready, r * RING + (k - 1))
                nc.scalar.activation(sg[:, k % 2, :], a_bank[k % 2][:, 0:F], ACT.Silu).then_inc(silu_ready, 1)

            def tile_ht(r, k, fill=False):
                act.wait_ge(ht_full, r * RING + (k + 1))
                if not fill:
                    act.wait_ge(y_full, r * RING + (k - 1))
                nc.scalar.copy(ht[:, k % 2, :, :],
                               b_bank[k % 2][:, 0:F].rearrange("p (c n) -> p c n", c=2)).then_inc(ht_ready, 1)

            def slot(r, k, n=RING, end=False):
                if n >= 2 and not (end and k > NT % RING + 1):
                    tile_silu(r, k - 2, n < 4)
                if n >= 3 and not (end and k > NT % RING + 2):
                    tile_ht(r, k - 3, n < 5)
                if not end:
                    tile_xt(r, k, n < 2)

            for k in range(RING):
                slot(0, k, k)
            with act.Fori(1, ROUNDS) as r:
                for k in range(RING):
                    slot(r, k)
            for k in range(NT % RING):
                slot(ROUNDS, k)
            for k in range(NT % RING, NT % RING + 3):
                slot(ROUNDS, k, end=True)

        @block.vector
        def _(dve):
            marks = [0]

            def mark(ins):
                marks[0] += 1
                ins.then_inc(v_chain, 1)
                return marks[0]

            def after(n):
                dve.wait_ge(v_chain, n)

            def link(ins):
                after(mark(ins))

            def reduce_chunk(u, i):
                block_, h0, n = CHUNKS[i]
                w, c = width(block_), NC * u + i
                dve.wait_ge(a_full, c + 1)
                nc.vector.tensor_reduce(mx[:, u % 2, block_, h0:h0 + n],
                                        a_ring[c % len(a_ring)][:, 0:n * w].rearrange("p (j w) -> p j w", j=n),
                                        AX.X, ALU.max).then_inc(a_read, 1)

            split_mark = [0]

            def split_maxima(u, i):
                m = mx[:, u % 2, :, :]
                if i > 0:
                    after(split_mark[0])
                if i == 0:
                    dve.wait_ge(a_read, NC * (u + 1))
                    if u > 0:
                        dve.wait_ge(p0_full, p0("mt", u - 1) + 1)
                    ins = nc.vector.tensor_scalar(mparts[:, :, 0, :], m, -1.0, None, ALU.mult)
                elif i == 1:
                    ins = nc.vector.scalar_tensor_tensor(out=mres[:, :, :], in0=m, scalar=-1.0,
                                                         in1=mparts[:, :, 0, :], op0=ALU.mult, op1=ALU.subtract)
                elif i == 2:
                    ins = nc.vector.tensor_copy(mparts[:, :, 1, :], mres[:, :, :])
                else:
                    nc.vector.tensor_tensor(mparts[:, :, 2, :], mres[:, :, :], mparts[:, :, 1, :],
                                            ALU.subtract).then_inc(mparts_ready, 1)
                    return
                split_mark[0] = mark(ins)

            def ln_stats(n, which, part):
                k = LAYERNORMS.index((n, which))
                if part == 0:
                    if which == 0:
                        dve.wait_ge(x_in_sem[n], 16)
                    for t in range(TB):
                        m = mark(nc.vector.bn_stats(stats[:, t, :], x[:, n * TB + t, :]))
                    stats_mark[0] = m
                    return
                after(stats_mark[0])
                if k >= 2:
                    m, w = LAYERNORMS[k - 2]
                    dve.wait_ge((xn1_ready, xn2_ready)[w], m + 1)
                for t in range(TB):
                    m = mark(nc.vector.bn_aggr(mv[:, k % 2, t, :], stats[:, t, :]))
                after(m)
                nc.vector.tensor_scalar(var[:, k % 2, :], mv[:, k % 2, :, 1], EPS, None, ALU.add).then_inc(var_ready, 1)

            stats_mark = [0]

            def ln_apply(n, which):
                k = LAYERNORMS.index((n, which))
                dve.wait_ge(rstd_ready, k + 1)
                to, ready = (xn1, xn1_ready) if which == 0 else (xn2, xn2_ready)
                if n > 0:
                    if which == 0:
                        dve.wait_ge(p0_full, p0("xn1t", n - 1) + 1)
                    else:
                        dve.wait_ge(rows_ready, n)
                for t in range(TB):
                    ins = nc.vector.tensor_scalar(to[:, t, :], x[:, n * TB + t, :], mv[:, k % 2, t, 0:1],
                                                  rstd[:, k % 2, t:t + 1], ALU.subtract, ALU.mult)
                ins.then_inc(ready, 1)

            def rope(n, i):
                qk, part = divmod(i, 2)
                dve.wait_ge(p1_full, p1("proj", (n, i)) + 1)
                if n > 0 and part == 0:
                    dve.wait_ge(split_ready, 2 * n)
                nc.vector.tensor_tensor((t1, t2)[part][:, qk, :], p1_bank[:, :], rot_sb[:, part, :],
                                        ALU.mult).then_inc(p1_read, 1)

            def rope_first(n, i):
                qk, part = divmod(i, 2)
                full, read, banks = ((proj0_full, proj0_read, proj0_bank), (proj1_full, proj1_read, proj1_bank))[n]
                dve.wait_ge(full, i + 1)
                if n > 0 and part == 0:
                    dve.wait_ge(split_ready, qk + 1)
                nc.vector.tensor_tensor((t1, t2)[part][:, qk, :], banks[i][:, :], rot_sb[:, part, :],
                                        ALU.mult).then_inc(read, 1)

            def rest0(qk, i):
                a, r = t1[:, qk, :], t2[:, qk, :]
                c = 3 * qk
                if i == 0:
                    dve.wait_ge(proj0_read, 2 * qk + 2)
                    nc.vector.tensor_tensor(a, a, r, ALU.add).then_inc(rest_ready, 1)
                elif i == 1:
                    dve.wait_ge(part_cast, qk + 1)
                    nc.vector.tensor_tensor(r, a, parts[:, c, :], ALU.subtract).then_inc(rest_ready, 1)
                else:
                    dve.wait_ge(part_cast, qk + 3)
                    nc.vector.tensor_tensor(parts[:, c + 2, :], r, parts[:, c + 1, :],
                                            ALU.subtract).then_inc(split_ready, 1)

            def normalise(u):
                b, g = divmod(u, UB)
                dve.wait_ge(p1_full, p1("ott", u) + 1)
                v = p1_bank[:, :].rearrange("p (t j c) -> p t j c", t=TB, c=VC)
                link(nc.vector.reciprocal(rc[:, :, :], v[:, :, :, D]))
                if g == 0 and b > 0:
                    dve.wait_ge(p0_full, p0("attnt", b - 1) + 1)
                nc.vector.tensor_tensor(
                    attn[:, :, g * HU * D:(g + 1) * HU * D].rearrange("p t (j d) -> p t j d", d=D),
                    v[:, :, :, 0:D], rc[:, :, :].unsqueeze(3).broadcast_to([P, TB, HU, D]),
                    ALU.mult).then_inc(norm_done, 1)
                dve.wait_ge(norm_done, u + 1)
                dve.sem_inc(p1_read, 1)

            def residual(b):
                dve.wait_ge(p1_full, p1("wo", b) + 1)
                xs = x[:, b * TB:(b + 1) * TB, :]
                nc.vector.tensor_tensor(xs, xs, p1_bank[:, :].rearrange("p (t e) -> p t e", e=E),
                                        ALU.add).then_inc(p1_read, 1)

            def route(b):
                dve.wait_ge(p1_full, p1("logits", b) + 1)
                dve.wait_ge(c_loaded, 48)
                nc.vector.tensor_copy(lg[:, :, :], p1_bank[:, 0:TB * NE].rearrange("p (t e) -> p t e", e=NE)
                                      ).then_inc(p1_read, 1)
                dve.wait_ge(p1_read, p1("logits", b) + 1)
                if b > 0:
                    dve.wait_ge(tanh_ready, b)
                nc.vector.tensor_reduce(mx4[:, :], lg[:, :, :], AX.X, ALU.max).then_inc(mx4_ready, 1)
                dve.wait_ge(mx4_ready, b + 1)
                link(nc.vector.tensor_tensor(eq[:, :, :], lg[:, :, :],
                                             mx4[:, :].unsqueeze(2).broadcast_to([P, TB, NE]), ALU.is_equal))
                link(nc.vector.tensor_tensor(eq[:, :, :], eq[:, :, :],
                                             ties.unsqueeze(1).broadcast_to([P, TB, NE]), ALU.mult))
                link(nc.vector.tensor_reduce(c4[:, :], eq[:, :, :], AX.X, ALU.max))
                nc.vector.tensor_tensor(onehot[:, b * TB:(b + 1) * TB, :], eq[:, :, :],
                                        c4[:, :].unsqueeze(2).broadcast_to([P, TB, NE]),
                                        ALU.is_equal).then_inc(onehot_ready, 1)

            place_mark = [0]

            def place(b, part):
                def over_tiles(v):
                    return v[:, :].unsqueeze(1).broadcast_to([P, TB, NE])

                if part == 0:
                    dve.wait_ge(p1_full, p1("rank", b) + 1)
                    if b == 0:
                        dve.wait_ge(books_cleared, 6)
                    r = p1_bank[:, 0:(TB + 1) * NE].rearrange("p (t e) -> p t e", e=NE)
                    nc.vector.tensor_tensor(rk[:, :, :], r[:, 0:TB, :], over_tiles(start), ALU.add)
                    nc.vector.tensor_tensor(past[:, :, :], r[:, 0:TB, :], over_tiles(room), ALU.is_ge)
                    nc.vector.tensor_tensor(count[:, :], r[:, TB, :], count[:, :], ALU.add).then_inc(p1_read, 1)
                    return
                if part == 1:
                    dve.wait_ge(p1_read, p1("rank", b) + 1)
                    ins = nc.vector.tensor_tensor(pair[:, :, :], count[:, :].unsqueeze(2).broadcast_to([P, NE, NE]),
                                                  full.unsqueeze(1).broadcast_to([P, NE, NE]), ALU.is_gt)
                else:
                    after(place_mark[0])
                if part == 2:
                    ins = nc.vector.tensor_reduce(tiles_new[:, :], pair[:, :, :], AX.X, ALU.add)
                elif part == 3:
                    link(nc.vector.tensor_tensor(added[:, :], tiles_new[:, :], tiles[:, :], ALU.subtract))
                    ins = nc.vector.tensor_tensor(pair[:, :, :], added[:, :].unsqueeze(1).broadcast_to([P, NE, NE]),
                                                  upto, ALU.mult)
                elif part == 4:
                    ins = nc.vector.tensor_reduce(ends[:, :], pair[:, :, :], AX.X, ALU.add)
                elif part == 5:
                    link(nc.vector.tensor_scalar(ends[:, :], ends[:, :], end_row[:, 0:1], None, ALU.add))
                    ins = nc.vector.scalar_tensor_tensor(out=shift_new[:, :], in0=tiles_new[:, :], scalar=-float(P),
                                                         in1=ends[:, :], op0=ALU.mult, op1=ALU.add)
                elif part == 6:
                    link(nc.vector.tensor_tensor(dshift[:, :], shift_new[:, :], shift[:, :], ALU.subtract))
                    ins = nc.vector.tensor_tensor(past[:, :, :], past[:, :, :], over_tiles(dshift), ALU.mult)
                elif part == 7:
                    link(nc.vector.tensor_tensor(rk[:, :, :], rk[:, :, :], past[:, :, :], ALU.add))
                    ins = nc.vector.tensor_tensor(rk[:, :, :], rk[:, :, :], onehot[:, b * TB:(b + 1) * TB, :],
                                                  ALU.mult)
                elif part == 8:
                    link(nc.vector.tensor_reduce(posf[:, :], rk[:, :, :], AX.X, ALU.add))
                    nc.vector.tensor_copy(posi[:, b * TB:(b + 1) * TB], posf[:, :]).then_inc(pos_ready, 1)
                    return
                elif part == 9:
                    ins = nc.vector.tensor_tensor(cmpt[:, :, :], ends[0:1, :].unsqueeze(1).broadcast_to([1, NT, NE]),
                                                  tile_row.unsqueeze(2).broadcast_to([1, NT, NE]), ALU.is_le)
                elif part == 10:
                    ins = nc.vector.tensor_reduce(exps[:, :] if b else expf[:, :], cmpt[:, :, :], AX.X, ALU.add)
                    if b > 0:
                        link(ins)
                        ins = nc.vector.tensor_tensor(expf[:, :], expf[:, :], exps[:, :], ALU.add)
                    if b == LAST:
                        link(ins)
                        link(nc.vector.tensor_copy(expi[:, :], expf[:, :]))
                        nc.vector.tensor_scalar(expi[:, :], expi[:, :], NE - 1, None,
                                                ALU.bitwise_and).then_inc(experts_ready, 1)
                        return
                elif part == 11:
                    nc.vector.tensor_copy(end_row[:, :], ends[:, NE - 1:NE])
                    nc.vector.tensor_copy(tiles[:, :], tiles_new[:, :])
                    ins = nc.vector.tensor_scalar(grown[:, :], added[:, :], 0.0, None, ALU.is_gt)
                elif part == 12:
                    link(nc.vector.tensor_tensor(grown[:, :], grown[:, :], dshift[:, :], ALU.mult))
                    ins = nc.vector.tensor_tensor(shift[:, :], shift[:, :], grown[:, :], ALU.add)
                elif part == 13:
                    nc.vector.tensor_tensor(start[:, :], count[:, :], shift[:, :], ALU.add)
                    ins = nc.vector.scalar_tensor_tensor(out=room[:, :], in0=tiles_new[:, :], scalar=float(P),
                                                         in1=count[:, :], op0=ALU.mult, op1=ALU.subtract)
                place_mark[0] = mark(ins)

            def expert_scale(b):
                dve.wait_ge(tanh_ready, b + 1)
                if b > 0:
                    dve.wait_ge(rows_ready, b)
                nc.vector.tensor_scalar(sg4[:, :], th[:, :], 0.5, 0.5, ALU.mult, ALU.add).then_inc(sg4_ready, 1)

            def expert_rows(b):
                dve.wait_ge(sg4_ready, b + 1)
                nc.vector.tensor_tensor(rows[:, b * TB:(b + 1) * TB, 0:E], xn2[:, :, :],
                                        sg4[:, :].unsqueeze(2).broadcast_to([P, TB, E]),
                                        ALU.mult).then_inc(last_rows_ready, 1)

            nc.vector.memset(ots[:, :], 0.0).then_inc(ots_cleared, 1)
            nc.vector.memset(half[:, :], -0.5).then_inc(half_done, 1)
            for book in (count, tiles, shift, room, start, end_row):
                nc.vector.memset(book[:, :], 0.0).then_inc(books_cleared, 1)
            nc.vector.memset(vaug[:, :, :, :], 0.0).then_inc(vones_done, 1)
            for n in range(2):
                ln_stats(n, 0, 0)
                ln_stats(n, 0, 1)
            ln_apply(0, 0)
            dve.wait_ge(vones_done, 1)
            nc.vector.memset(vaug[:, :, :, D], 1.0).then_inc(vones_done, 1)
            ln_apply(1, 0)
            dve.wait_ge(rot_loaded, 16)
            rope_first(0, 0)
            rope_first(0, 1)
            rest0(0, 0)
            rope_first(0, 2)
            rope_first(0, 3)
            rest0(1, 0)
            for i in range(1, 3):
                for qk in range(2):
                    rest0(qk, i)
            for i in range(4):
                rope_first(1, i)
            for i in range(NC):
                reduce_chunk(0, i)
            for i in range(4):
                split_maxima(0, i)
            for i in range(NC):
                reduce_chunk(1, i)
            for u in range(U):
                b, g = divmod(u, UB)
                todo = extras(u)
                for i in range(NC):
                    if u + 2 < U:
                        reduce_chunk(u + 2, i)
                    if u + 1 < U and i < 4:
                        split_maxima(u + 1, i)
                    for at, name, arg in todo:
                        if min(at + 1, NC - 1) != i:
                            continue
                        if name == "proj":
                            rope(*arg)
                        elif name == "ott":
                            normalise(arg)
                        elif name == "wo":
                            residual(arg)
                        elif name == "logits":
                            route(arg)
                        elif name == "early":
                            dve.wait_ge(early_full, arg + 1)
                            if arg == 0:
                                dve.wait_ge(parts_sent, 96 * B)
                                dve.wait_ge(v_copied, B)
                            nc.vector.tensor_copy(early_sb[arg], a_ring[arg % len(a_ring)][:, :]
                                                  ).then_inc(early_read, 1)
                    if g == 1 and b > 0 and i < 2:
                        if i == 0:
                            dve.wait_ge(p1_read, p1("wo", b - 1) + 1)
                        ln_stats(b - 1, 1, i)
                    if g == 2 and b > 0 and i >= 4:
                        place(b - 1, i - 4)
                    if g == 3 and b > 0 and i < 7:
                        place(b - 1, i + 7)
                    if g == 2 and b > 0 and i == 5:
                        expert_scale(b - 1)
                    if g == 1 and b + 2 < B and i in (7, 8):
                        ln_stats(b + 2, 0, i - 7)
            for name, arg in TAIL:
                if name == "ott":
                    normalise(arg)
                elif name == "wo":
                    residual(arg)
                    dve.wait_ge(p1_read, p1("wo", arg) + 1)
                    ln_stats(arg, 1, 0)
                    ln_stats(arg, 1, 1)
                elif name == "norm2":
                    ln_apply(arg, 1)
                elif name == "logits":
                    route(arg)
                elif name == "place":
                    for part in arg:
                        place(LAST, part)
                elif name == "expert_rows":
                    expert_scale(arg)
                    expert_rows(arg)
                elif name == "mul":
                    b, c = arg
                    dve.wait_ge(sh_silu, 2 * b + c + 1)
                    if b < EARLY // 4:
                        ups = early_sb[4 * b + 2 + c]
                        dve.wait_ge(early_read, EARLY)
                    else:
                        ups = b_bank[c][:, :]
                        dve.wait_ge(up_full, 2 * (b - EARLY // 4) + c + 1)
                    if b > 1:
                        dve.wait_ge(down_full, b - 1)
                    nc.vector.tensor_tensor(shh[:, b % 2, c, :], ups, shg[:, c, :],
                                            ALU.mult).then_inc(sh_mul, 1)
                elif name == "add":
                    b = arg
                    if b < LAST:
                        dve.wait_ge(down_full, b + 1)
                        xs = x[:, b * TB:(b + 1) * TB, :]
                        nc.vector.tensor_tensor(xs, xs, b_bank[2][:, :].rearrange("p (t e) -> p t e", e=E),
                                                ALU.add).then_inc(base_done, 1)
                    else:
                        for t in range(TB):
                            dve.wait_ge(down_full, b + t + 1)
                            xs = x[:, b * TB + t, :]
                            nc.vector.tensor_tensor(xs, xs, last_banks[t][:, t * P:(t + 1) * P],
                                                    ALU.add).then_inc(base_done, 1)

            def tile_mul(r, k, fill=False):
                dve.wait_ge(silu_ready, r * RING + (k + 1))
                if not fill:
                    dve.wait_ge(ht_full, r * RING + (k - 1))
                nc.vector.tensor_tensor(hh[:, k % 2, :], a_bank[k % 2][:, F:2 * F], sg[:, k % 2, :],
                                        ALU.mult).then_inc(hh_ready, 1)

            def tile_y(r, k, fill=False):
                dve.wait_ge(y_full, r * RING + (k + 1))
                if not fill:
                    dve.wait_ge(y_sent[k % YRING], 16 * (r * (RING // YRING) + k // YRING))
                nc.vector.tensor_tensor(yt[:, k % YRING, :], [b_bank[2], ot_bank][k % 2][:, 0:E],
                                        xin[:, k % RING, E:2 * E], ALU.add).then_inc(y_ready, 1)

            def slot(r, k, n=RING, end=False):
                if n >= 2 and not (end and k > NT % RING + 1):
                    tile_mul(r, k - 2, n < 4)
                if n >= 4:
                    tile_y(r, k - 4, n < 4 + YRING and r == 0)

            for k in range(RING):
                slot(0, k, k)
            with dve.Fori(1, ROUNDS) as r:
                for k in range(RING):
                    slot(r, k)
            for k in range(NT % RING):
                slot(ROUNDS, k)
            for k in range(NT % RING, NT % RING + 4):
                slot(ROUNDS, k, end=True)

        @block.gpsimd
        def _(pool):
            step = [0]
            ln = [0]

            def root():
                k = ln[0]
                ln[0] += 1
                pool.wait_ge(half_done, 1)
                pool.wait_ge(var_ready, k + 1)
                nc.gpsimd.tensor_tensor(rstd[:, k % 2, :], var[:, k % 2, :], half[:, :], ALU.pow).then_inc(rstd_ready, 1)

            def ln_apply(n, which):
                k = LAYERNORMS.index((n, which))
                to, ready = (xn1, xn1_ready) if which == 0 else (xn2, xn2_ready)
                pool.wait_ge(rstd_ready, k + 1)
                if which == 0:
                    pool.wait_ge(p0_full, p0("xn1t", n - 1) + 1)
                elif n > 0:
                    pool.wait_ge(rows_ready, n)
                nc.gpsimd.tensor_tensor(to[:, :, :], x[:, n * TB:(n + 1) * TB, :],
                                        mv[:, k % 2, :, 0:1].broadcast_to([P, TB, E]),
                                        ALU.subtract).then_inc(centred, 1)
                pool.wait_ge(centred, k - 1)
                nc.gpsimd.tensor_tensor(to[:, :, :], to[:, :, :],
                                        rstd[:, k % 2, :].unsqueeze(2).broadcast_to([P, TB, E]),
                                        ALU.mult).then_inc(ready, 1)

            def expert_rows(b):
                pool.wait_ge(sg4_ready, b + 1)
                pool.wait_ge(xn2_ready, b + 1)
                pool.wait_ge(ids_done, 1)
                nc.gpsimd.tensor_tensor(rows[:, b * TB:(b + 1) * TB, 0:E], xn2[:, :, :],
                                        sg4[:, :].unsqueeze(2).broadcast_to([P, TB, E]),
                                        ALU.mult).then_inc(rows_ready, 1)

            def split(n, qk, i):
                a, r = t1[:, qk, :], t2[:, qk, :]
                c = 3 * qk
                if i == 0 and n == 1:
                    pool.wait_ge(proj1_read, 2 * qk + 2)
                elif i == 0:
                    pool.wait_ge(p1_read, p1("proj", (n, 2 * qk + 1)) + 1)
                else:
                    pool.wait_ge(split_step, step[0])
                if i == 0:
                    ins = nc.gpsimd.tensor_tensor(a, a, r, ALU.add)
                elif i == 1:
                    pool.wait_ge(parts_sent, 96 * n)
                    ins = nc.gpsimd.tensor_copy(parts[:, c, :], a)
                elif i == 2:
                    ins = nc.gpsimd.tensor_tensor(r, a, parts[:, c, :], ALU.subtract)
                elif i == 3:
                    ins = nc.gpsimd.tensor_copy(parts[:, c + 1, :], r)
                else:
                    nc.gpsimd.tensor_tensor(parts[:, c + 2, :], r, parts[:, c + 1, :],
                                            ALU.subtract).then_inc(split_ready, 1)
                    return
                ins.then_inc(split_step, 1)
                step[0] += 1

            def select(u, kt):
                w, off = S - kt * P, PT_OFF[kt]
                pool.wait_ge(b_read, NC * u + LAST_CHUNK[kt] + 1)
                v = pt[:, u % 2, off:off + HU * w].rearrange("p (j w) -> p j w", j=HU)[:, :, 0:P]
                nc.gpsimd.affine_select(out=v, in_=v, pattern=[[0, HU], [1, P]], compare_op=ALU.is_ge,
                                        fill=fill, base=0, channel_multiplier=-1).then_inc(masked, 1)

            fill = pool.to_reg(0.0)
            root()
            root()
            pool.wait_ge(rstd_ready, 2)
            nc.gpsimd.memset(kst[32:64, :, :].bitcast(I32), 0).then_inc(zeros_done, 1)
            pool.wait_ge(zeros_done, 1)
            nc.gpsimd.memset(qst[32:64, :, :].bitcast(I32), 0).then_inc(zeros_done, 1)
            pool.wait_ge(zeros_done, 2)
            nc.gpsimd.iota(rows[:, :, 2 * E:ROW].bitcast(I32), [[P, T]], base=0, channel_multiplier=1).then_inc(ids_done, 1)
            nc.gpsimd.memset(zrow[:, 0:2 * E], 0.0).then_inc(zrow_done, 1)
            nc.gpsimd.memset(zrow[:, 2 * E:ROW].bitcast(I32), NOBODY).then_inc(zrow_done, 1)
            for qk in range(2):
                for i in range(5):
                    split(1, qk, i)
            for u in range(U):
                b, g = divmod(u, UB)
                if g == 1 and b > 0:
                    root()
                n, qk = (b + 2, 0) if g == 3 else (b + 1, 1)
                splits = g in (0, 3) and 2 <= n < B
                select(u, 0)
                if splits:
                    for i in range(3):
                        split(n, qk, i)
                if g == 1 and b > 0:
                    ln_apply(b - 1, 1)
                if g == 2 and b + 2 < B:
                    ln_apply(b + 2, 0)
                select(u, 1)
                if splits:
                    for i in range(3, 5):
                        split(n, qk, i)
                if g == 2 and b > 0:
                    expert_rows(b - 1)
                select(u, 2)
                if g == 1 and b + 2 < B:
                    root()
                select(u, 3)
            bound = pool.to_reg(NT * P - 1)
            token_bound = pool.to_reg(B * S - 1)
            pool.wait_ge(table_cleared, 16 * UB * 2)
            for t in range(T):
                if t == SCATTERS_BEFORE_ROOT:
                    root()
                if t % TB == 0:
                    if t // TB < LAST:
                        pool.wait_ge(rows_ready, t // TB + 1)
                    else:
                        pool.wait_ge(last_rows_ready, 1)
                    pool.wait_ge(pos_ready, t // TB + 1)
                if t // TB == LAST:
                    pool.wait_ge(base_done, LAST + t % TB + 1)
                elif t % TB == 0:
                    pool.wait_ge(base_done, t // TB + 1)
                nc.gpsimd.indirect_dma_start(rows_scr.ap(), bass.IndirectOffsetOnAxis(ap=posi[:, t:t + 1], axis=0),
                                             rows[:, t, :], None, bounds_check=bound,
                                             oob_is_err=False).then_inc(scattered, 16)
            for i in range(NT):
                pool.wait_ge(y_ready, i + 1)
                ids = xin[:, i % RING, 2 * E:ROW].bitcast(I32)
                nc.gpsimd.indirect_dma_start(out_rows, bass.IndirectOffsetOnAxis(ap=ids, axis=0),
                                             yt[:, i % YRING, :], None, bounds_check=token_bound,
                                             oob_is_err=False).then_inc(y_sent[i % YRING], 16)


def constants():
    import numpy as np
    f4, bf = np.float32, mybir.dt.np(BF16)
    inv = (1.0 / (f4(10000.0) ** (np.arange(0, D, 2, dtype=f4) / f4(D)))).astype(f4)
    freqs = np.outer(np.arange(S, dtype=f4), inv).astype(f4)
    emb = np.concatenate([freqs, freqs], -1)
    sign = np.where(np.arange(D) % 2 == 0, -1.0, 1.0).astype(f4)
    cos = np.repeat(np.cos(emb).T.astype(f4), H, axis=0)
    sin = np.repeat((np.sin(emb) * sign).T.astype(f4), H, axis=0)
    i = np.arange(P)
    mask = np.where(i[None, :] > i[:, None], -1e30, 0.0)
    ident_mask = np.stack([np.eye(P)] + [mask] * HU, axis=1).astype(bf)
    sel = np.zeros((3, HU, UB, HU, S))
    for j in range(HU):
        sel[:, j, :, j, :] = 1.0
    sel = sel.reshape(3 * HU, H, S).astype(bf)
    rank = np.zeros((P, 3 * P))
    rank[:, 0:P] = i[:, None] < i[None, :]
    rank[:, P:2 * P] = 1.0
    e = np.arange(NE)
    upto = P * (e[None, :] <= e[:, None])
    small = np.concatenate([NE - e, P * e, upto.reshape(-1), P * np.arange(NT)]).astype(f4)
    small = np.repeat(small[None, :], P, axis=0)
    return {
        "rot": np.stack([cos, sin], axis=1), "ident": np.eye(P, dtype=f4), "ident_mask": ident_mask,
        "sel": sel, "rank": rank.astype(bf), "small": small,
    }


def kernel(L0_attn_x, L0_attn_Wq, L0_attn_Wk, L0_attn_Wv, L0_attn_Wo, L0_ffn_w_router, L0_ffn_gate_up_proj,
           L0_ffn_down_proj, L0_ffn_w_gate, L0_ffn_w_up, L0_ffn_w_down):
    import numpy as np
    import concourse.bacc as bacc
    from concourse.bass_utils import run_bass_kernel_spmd

    d_h = np.arange(H * D).reshape(H, D).T.reshape(-1)
    swapped = (np.arange(H * D) ^ 1).reshape(H, D).T.reshape(-1)
    wq, wk = np.asarray(L0_attn_Wq), np.asarray(L0_attn_Wk)
    c = constants()
    arrays = {
        "x": np.asarray(L0_attn_x),
        "w_att": np.stack([wq[d_h].T, wq[swapped].T, wk[d_h].T, wk[swapped].T,
                           np.asarray(L0_attn_Wv).T, np.asarray(L0_attn_Wo).T], axis=1),
        "w_router": np.asarray(L0_ffn_w_router).T,
        "w_gu": np.asarray(L0_ffn_gate_up_proj), "w_dn": np.asarray(L0_ffn_down_proj),
        "w_sh": np.concatenate([np.asarray(L0_ffn_w_gate).T, np.asarray(L0_ffn_w_up).T], axis=1),
        "w_shd": np.asarray(L0_ffn_w_down).T,
        **c,
    }
    arrays = {"in_" + k: np.ascontiguousarray(v) for k, v in arrays.items()}
    nc = bacc.Bacc("TRN2", target_bir_lowering=False, num_devices=1)
    args = [nc.dram_tensor(k, v.shape, mybir.dt.from_np(v.dtype), kind="ExternalInput").ap()
            for k, v in arrays.items()]
    out = nc.dram_tensor("out", (B, S, E), F32, kind="ExternalOutput").ap()
    block_kernel(nc, *args, out)
    result = run_bass_kernel_spmd(nc, [arrays], core_ids=[0])
    return result.results[0]["out"]
```
